# Optimizing a Trainium2 kernel written in Bass

```python
import numpy as np
import jax
import jax.numpy as jnp

def _softmax(x, axis=-1):
    return jax.nn.softmax(x, axis=axis)

def _gelu(x):
    return jax.nn.gelu(x, approximate=True)

def _silu(x):
    return jax.nn.silu(x)

def _sigmoid(x):
    return jax.nn.sigmoid(x)

def _layernorm(x, axis=-1, eps=1e-05):
    m = jnp.mean(x, axis=axis, keepdims=True)
    v = jnp.var(x, axis=axis, keepdims=True)
    return (x - m) / jnp.sqrt(v + eps)

def _scatter_add(tgt, idx, src, axis=0):
    return tgt.at[idx].add(src)

def _segment_sum(src, seg, n):
    return jax.ops.segment_sum(src, seg, n)
kernel_name = 'mk_adaln_ffn_d1_seqx_r8_4e543e'

def setup_inputs(seed: int=0):
    np.random.seed(seed)
    _w = jnp.asarray

    def _rec_inputs():
        import jax
        import jax.numpy as jnp
        _rk = jax.random.key(seed)
        x = -0.0003929 + 0.9999 * jax.random.normal(jax.random.fold_in(_rk, 1), (128, 32, 128), jnp.float32)
        _lenS = 32 - jax.random.randint(jax.random.fold_in(_rk, 7), (128,), 0, max(1, 32 // 4) + 1, jnp.int32)
        _lenS2 = 32 - jax.random.randint(jax.random.fold_in(_rk, 8), (128,), 0, max(1, 32 // 4) + 1, jnp.int32)
        itok_B_0_2 = jax.random.randint(jax.random.fold_in(_rk, 11), (128,), 0, 3, jnp.int32)
        return (x, itok_B_0_2)
    x, itok_B_0_2 = _rec_inputs()

    def _L0_cond_setup():
        import jax, jax.numpy as jnp
        import numpy as np
        B, S, D, F, E = (8, 256, 128, 512, 5)

        def _dense(x, wi_, wo_):
            return jax.nn.relu(x @ wi_) @ wo_
        key = jax.random.key(seed)
        ks = jax.random.split(key, 9)
        sc = 0.02
        return {'hidden_states': jax.random.normal(ks[0], (B, S, D), jnp.float32), 'type_label': jax.random.randint(ks[1], (B,), 0, E, jnp.int32), 'wi': jax.random.normal(ks[2], (E, D, F), jnp.float32) * sc, 'wo': jax.random.normal(ks[3], (E, F, D), jnp.float32) * sc, 'swi': jax.random.normal(ks[4], (2, D, F), jnp.float32) * sc, 'swo': jax.random.normal(ks[5], (2, F, D), jnp.float32) * sc, 'g1': jax.random.normal(ks[6], (3 * D, D), jnp.float32) * sc, 'g2': jax.random.normal(ks[7], (D, 3), jnp.float32) * sc}
    _L0_cond_all = _L0_cond_setup()
    _L0_cond_in = {k: v for k, v in _L0_cond_all.items() if k in ('wi', 'wo', 'swi', 'swo', 'g1', 'g2')}
    del _L0_cond_all

    def _L0_ffn_setup():
        import jax, jax.numpy as jnp
        import numpy as np
        DIM = 128
        DEPTH = 6
        HEADS = 16
        DIM_HEAD = 64
        WINDOW = 32
        INNER = HEADS * DIM_HEAD
        DIM_INNER = int(DIM * 4 * 2 / 3)
        QK_SCALE = 8.0

        def shift_tokens(t):
            a, s = jnp.split(t, 2, -1)
            s = jnp.pad(s, ((0, 0), (1, 0), (0, 0)))[:, :-1]
            return jnp.concatenate([a, s], -1)

        def l2norm(t):
            return t / jnp.maximum(jnp.linalg.norm(t, axis=-1, keepdims=True), 1e-12)

        def rotate_half(x):
            x1, x2 = jnp.split(x, 2, -1)
            return jnp.concatenate([-x2, x1], -1)

        def rotary_tables(n):
            half = jnp.arange(0, DIM_HEAD, 2, dtype=jnp.float32)
            inv_freq = 1.0 / 10000.0 ** (half / DIM_HEAD)
            t = jnp.arange(n, dtype=jnp.float32)
            freqs = t[:, None] * inv_freq[None, :]
            freqs = jnp.concatenate([freqs, freqs], -1)
            base_scale = (half + 0.4 * DIM_HEAD) / (1.4 * DIM_HEAD)
            power = (t - n // 2) / (WINDOW // 2)
            scale = base_scale[None, :] ** power[:, None]
            scale = jnp.concatenate([scale, scale], -1)
            return (freqs, scale)

        def local_attention(q, k, v):
            b, h, n, d = q.shape
            w = WINDOW
            nw = n // w
            bq = q.reshape(b, h, nw, w, d)
            bk = k.reshape(b, h, nw, w, d)
            bv = v.reshape(b, h, nw, w, d)

            def look(t):
                p = jnp.pad(t, ((0, 0), (0, 0), (1, 0), (0, 0), (0, 0)))
                return jnp.concatenate([p[:, :, :nw], p[:, :, 1:]], axis=3)
            bk2, bv2 = (look(bk), look(bv))
            seq = jnp.arange(n).reshape(nw, w)
            seq_p = jnp.pad(seq, ((1, 0), (0, 0)), constant_values=-1)
            jt = jnp.concatenate([seq_p[:nw], seq_p[1:]], axis=1)
            it = seq[:, :, None]
            jb = jt[:, None, :]
            mask = (it < jb) | (it > jb + w) | (jb == -1)
            sim = jnp.einsum('bhwie,bhwje->bhwij', bq, bk2) * QK_SCALE
            sim = jnp.where(mask, -jnp.finfo(sim.dtype).max, sim)
            attn = jax.nn.softmax(sim, -1)
            out = jnp.einsum('bhwij,bhwje->bhwie', attn, bv2)
            return out.reshape(b, h, n, d)

        def attn_layer(x, Wqkv, qs, ksc, Wo):
            b, n, _ = x.shape
            qkv = x @ Wqkv
            q, k, v = jnp.split(qkv, 3, -1)
            sh = lambda t: t.reshape(b, n, HEADS, DIM_HEAD).transpose(0, 2, 1, 3)
            q, k, v = (sh(q), sh(k), sh(v))
            q = l2norm(q) * qs
            k = l2norm(k) * ksc
            freqs, scale = rotary_tables(n)
            cos, sin = (jnp.cos(freqs), jnp.sin(freqs))
            q = q * cos * scale + rotate_half(q) * sin * scale
            inv = 1.0 / scale
            k = k * cos * inv + rotate_half(k) * sin * inv
            out = local_attention(q, k, v)
            out = out.transpose(0, 2, 1, 3).reshape(b, n, INNER)
            return out @ Wo

        def ffn_layer(x, g, bln, W1, b1, W2, b2):
            mu = x.mean(-1, keepdims=True)
            var = ((x - mu) ** 2).mean(-1, keepdims=True)
            xn = (x - mu) / jnp.sqrt(var + 1e-05) * g + bln
            hg = xn @ W1 + b1
            a, gate = jnp.split(hg, 2, -1)
            return a * jax.nn.gelu(gate, approximate=False) @ W2 + b2
        key = jax.random.key(seed)
        ks = jax.random.split(key, 8)
        B, N = (2, 256)
        init = lambda k, shape: jax.random.normal(k, shape, jnp.float32) * 0.02
        return {'x': jax.random.normal(ks[0], (B, N, DIM), jnp.float32), 'Wqkv': init(ks[1], (DEPTH, DIM, 3 * INNER)), 'q_scale': jnp.ones((DEPTH, DIM_HEAD), jnp.float32), 'k_scale': jnp.ones((DEPTH, DIM_HEAD), jnp.float32), 'Wo': init(ks[2], (DEPTH, INNER, DIM)), 'ln_g': jnp.ones((DEPTH, DIM), jnp.float32), 'ln_b': jnp.zeros((DEPTH, DIM), jnp.float32), 'W1': init(ks[3], (DEPTH, DIM, 2 * DIM_INNER)), 'b1': jnp.zeros((DEPTH, 2 * DIM_INNER), jnp.float32), 'W2': init(ks[4], (DEPTH, DIM_INNER, DIM)), 'b2': jnp.zeros((DEPTH, DIM), jnp.float32)}
    _L0_ffn_all = _L0_ffn_setup()
    _L0_ffn_in = {k: v for k, v in _L0_ffn_all.items() if k in ('Wqkv', 'q_scale', 'k_scale', 'Wo', 'ln_g', 'ln_b', 'W1', 'b1', 'W2', 'b2')}
    del _L0_ffn_all
    return {'x': x, 'itok_B_0_2': itok_B_0_2, 'L0_cond_wi': _L0_cond_in['wi'], 'L0_cond_wo': _L0_cond_in['wo'], 'L0_cond_swi': _L0_cond_in['swi'], 'L0_cond_swo': _L0_cond_in['swo'], 'L0_cond_g1': _L0_cond_in['g1'], 'L0_cond_g2': _L0_cond_in['g2'], 'L0_ffn_Wqkv': _L0_ffn_in['Wqkv'], 'L0_ffn_q_scale': _L0_ffn_in['q_scale'], 'L0_ffn_k_scale': _L0_ffn_in['k_scale'], 'L0_ffn_Wo': _L0_ffn_in['Wo'], 'L0_ffn_ln_g': _L0_ffn_in['ln_g'], 'L0_ffn_ln_b': _L0_ffn_in['ln_b'], 'L0_ffn_W1': _L0_ffn_in['W1'], 'L0_ffn_b1': _L0_ffn_in['b1'], 'L0_ffn_W2': _L0_ffn_in['W2'], 'L0_ffn_b2': _L0_ffn_in['b2']}

def reference(x, itok_B_0_2, L0_cond_wi, L0_cond_wo, L0_cond_swi, L0_cond_swo, L0_cond_g1, L0_cond_g2, L0_ffn_Wqkv, L0_ffn_q_scale, L0_ffn_k_scale, L0_ffn_Wo, L0_ffn_ln_g, L0_ffn_ln_b, L0_ffn_W1, L0_ffn_b1, L0_ffn_W2, L0_ffn_b2):
    import jax
    import jax.numpy as jnp

    def _L0_cond_ref(hidden_states, type_label, wi, wo, swi, swo, g1, g2):
        import jax, jax.numpy as jnp
        import numpy as np
        B, S, D, F, E = (8, 256, 128, 512, 5)

        def _dense(x, wi_, wo_):
            return jax.nn.relu(x @ wi_) @ wo_
        x = hidden_states
        s0 = _dense(x, swi[0], swo[0])
        s1 = _dense(x, swi[1], swo[1])
        wi_sel = wi[type_label]
        wo_sel = wo[type_label]
        h = jax.nn.relu(jnp.einsum('bsd,bdf->bsf', x, wi_sel))
        eo = jnp.einsum('bsf,bfd->bsd', h, wo_sel)
        gate_in = jnp.concatenate([eo[:, 0], s0[:, 0], s1[:, 0]], axis=-1)
        w = jax.nn.softmax(jax.nn.relu(gate_in @ g1) @ g2, axis=-1)
        w = w[:, :, None, None]
        return eo * w[:, 0] + s0 * w[:, 1] + s1 * w[:, 2]

    def _L0_ffn_ref(x, Wqkv, q_scale, k_scale, Wo, ln_g, ln_b, W1, b1, W2, b2):
        import jax, jax.numpy as jnp
        import numpy as np
        DIM = 128
        DEPTH = 6
        HEADS = 16
        DIM_HEAD = 64
        WINDOW = 32
        INNER = HEADS * DIM_HEAD
        DIM_INNER = int(DIM * 4 * 2 / 3)
        QK_SCALE = 8.0

        def shift_tokens(t):
            a, s = jnp.split(t, 2, -1)
            s = jnp.pad(s, ((0, 0), (1, 0), (0, 0)))[:, :-1]
            return jnp.concatenate([a, s], -1)

        def l2norm(t):
            return t / jnp.maximum(jnp.linalg.norm(t, axis=-1, keepdims=True), 1e-12)

        def rotate_half(x):
            x1, x2 = jnp.split(x, 2, -1)
            return jnp.concatenate([-x2, x1], -1)

        def rotary_tables(n):
            half = jnp.arange(0, DIM_HEAD, 2, dtype=jnp.float32)
            inv_freq = 1.0 / 10000.0 ** (half / DIM_HEAD)
            t = jnp.arange(n, dtype=jnp.float32)
            freqs = t[:, None] * inv_freq[None, :]
            freqs = jnp.concatenate([freqs, freqs], -1)
            base_scale = (half + 0.4 * DIM_HEAD) / (1.4 * DIM_HEAD)
            power = (t - n // 2) / (WINDOW // 2)
            scale = base_scale[None, :] ** power[:, None]
            scale = jnp.concatenate([scale, scale], -1)
            return (freqs, scale)

        def local_attention(q, k, v):
            b, h, n, d = q.shape
            w = WINDOW
            nw = n // w
            bq = q.reshape(b, h, nw, w, d)
            bk = k.reshape(b, h, nw, w, d)
            bv = v.reshape(b, h, nw, w, d)

            def look(t):
                p = jnp.pad(t, ((0, 0), (0, 0), (1, 0), (0, 0), (0, 0)))
                return jnp.concatenate([p[:, :, :nw], p[:, :, 1:]], axis=3)
            bk2, bv2 = (look(bk), look(bv))
            seq = jnp.arange(n).reshape(nw, w)
            seq_p = jnp.pad(seq, ((1, 0), (0, 0)), constant_values=-1)
            jt = jnp.concatenate([seq_p[:nw], seq_p[1:]], axis=1)
            it = seq[:, :, None]
            jb = jt[:, None, :]
            mask = (it < jb) | (it > jb + w) | (jb == -1)
            sim = jnp.einsum('bhwie,bhwje->bhwij', bq, bk2) * QK_SCALE
            sim = jnp.where(mask, -jnp.finfo(sim.dtype).max, sim)
            attn = jax.nn.softmax(sim, -1)
            out = jnp.einsum('bhwij,bhwje->bhwie', attn, bv2)
            return out.reshape(b, h, n, d)

        def attn_layer(x, Wqkv, qs, ksc, Wo):
            b, n, _ = x.shape
            qkv = x @ Wqkv
            q, k, v = jnp.split(qkv, 3, -1)
            sh = lambda t: t.reshape(b, n, HEADS, DIM_HEAD).transpose(0, 2, 1, 3)
            q, k, v = (sh(q), sh(k), sh(v))
            q = l2norm(q) * qs
            k = l2norm(k) * ksc
            freqs, scale = rotary_tables(n)
            cos, sin = (jnp.cos(freqs), jnp.sin(freqs))
            q = q * cos * scale + rotate_half(q) * sin * scale
            inv = 1.0 / scale
            k = k * cos * inv + rotate_half(k) * sin * inv
            out = local_attention(q, k, v)
            out = out.transpose(0, 2, 1, 3).reshape(b, n, INNER)
            return out @ Wo

        def ffn_layer(x, g, bln, W1, b1, W2, b2):
            mu = x.mean(-1, keepdims=True)
            var = ((x - mu) ** 2).mean(-1, keepdims=True)
            xn = (x - mu) / jnp.sqrt(var + 1e-05) * g + bln
            hg = xn @ W1 + b1
            a, gate = jnp.split(hg, 2, -1)
            return a * jax.nn.gelu(gate, approximate=False) @ W2 + b2
        for i in range(DEPTH):
            x = attn_layer(shift_tokens(x), Wqkv[i], q_scale[i], k_scale[i], Wo[i]) + x
            x = ffn_layer(shift_tokens(x), ln_g[i], ln_b[i], W1[i], b1[i], W2[i], b2[i]) + x
        return x
    x = x + _L0_ffn_ref(_L0_cond_ref(x, itok_B_0_2, L0_cond_wi, L0_cond_wo, L0_cond_swi, L0_cond_swo, L0_cond_g1, L0_cond_g2), L0_ffn_Wqkv, L0_ffn_q_scale, L0_ffn_k_scale, L0_ffn_Wo, L0_ffn_ln_g, L0_ffn_ln_b, L0_ffn_W1, L0_ffn_b1, L0_ffn_W2, L0_ffn_b2)
    return x

_drawn_inputs = setup_inputs


def setup_inputs(seed=0):
    import zlib

    import numpy as np

    out = dict(_drawn_inputs(seed))
    spreads = {'L0_ffn_q_scale': (1.0, 0.6),
     'L0_ffn_k_scale': (1.0, 0.6),
     'L0_ffn_ln_g': (1.0, 0.6),
     'L0_ffn_ln_b': (0.0, 0.8),
     'L0_ffn_b1': (0.0, 0.436),
     'L0_ffn_b2': (0.0, 0.1)}
    factors = {'L0_cond_g1': 8.0, 'L0_cond_g2': 24.222}
    for name, (base, spread) in spreads.items():
        noise = np.random.default_rng([zlib.crc32(name.encode()), seed]).standard_normal(out[name].shape)
        drawn = base * np.exp(spread * noise) if base else spread * noise
        out[name] = jnp.asarray(drawn.astype(out[name].dtype))
    for name, factor in factors.items():
        out[name] = (out[name] * factor).astype(out[name].dtype)
    return out
```

```python
from contextlib import ExitStack, nullcontext

import concourse.bass as bass
from concourse import mybir

F32 = mybir.dt.float32
F32R = mybir.dt.float32r
BF16 = mybir.dt.bfloat16
I32 = mybir.dt.int32
ALU = mybir.AluOpType
ACT = mybir.ActivationFunctionType
AX_X = mybir.AxisListType.X

P = 128
BATCH, SEQ, DIM = 128, 32, 128
TOK = BATCH * SEQ
TILE = 128
TB = TILE // SEQ
GTOK = 512
GT = GTOK // TILE
GROUPS = TOK // GTOK
GB = GTOK // SEQ
LAYERS, HEADS, HD = 6, 16, 64
HP = HEADS // 2
INNER = HEADS * HD
DI = 341
FC = [(0, 128), (128, 128), (256, 85)]
EXPERTS, SHARED, EF = 5, 2, 512
EC = EF // P
TURNS = LAYERS * GROUPS
NEG = -1e30
LN_EPS = 1e-5
SS_SCALE = float(2 ** 20)
Y_SCALE = float(2 ** 10)
LN_EXP_SET = "natural_log_exp_and_others"
PG, PB, PB2, PBA, PBG, NPAR = 0, 1, 2, 3, 6, 9


def known(count):
    return max(count, 0) if isinstance(count, int) else count


def has_front(it):
    return not (isinstance(it, int) and it == TURNS)


def has_cd(it, j):
    if isinstance(it, int):
        return j >= 1 if it == 0 else j == 0
    return True


def has_ef(it, j):
    if isinstance(it, int):
        return j >= 2 if it == 0 else j < 2
    return True


def has_ffn(it):
    return not (isinstance(it, int) and it == 0)


def has_use(key, it):
    kind, j = key[0], key[1]
    if kind == "qkv":
        return has_front(it)
    if kind == "qkT":
        return has_cd(it, j)
    if kind in ("av", "wo"):
        return has_ef(it, j)
    return has_ffn(it)


def layer_of(it):
    layer = it >> 3
    return layer if isinstance(layer, int) else layer.with_bounds(min_val=0, max_val=LAYERS - 1)


def first_turn_of_layer(eng, it):
    return nullcontext() if isinstance(it, int) else eng.If((it & (GROUPS - 1)) < 1)


class Ring:

    def __init__(self, banks, keys):
        self.n, self.keys = banks, keys

    def bank(self, key):
        return self.keys.index(key) % self.n

    def nth(self, key, it):
        bank = self.bank(key)
        here = [k for k in self.keys[bank::self.n] if k is not None]
        upto = here[:here.index(key) + 1]
        first = sum(has_use(k, 0) for k in here)
        if isinstance(it, int) and it == 0:
            return sum(has_use(k, 0) for k in upto)
        if isinstance(it, int):
            return first + (TURNS - 1) * len(here) + sum(has_use(k, it) for k in upto)
        return it * len(here) + (first - len(here) + len(upto))


def a_ring_keys():
    keys = []
    for j in range(GT):
        keys += [("qkv", j, c) for c in range(6)]
        if j == 3:
            keys += [("up", j, c) for c in range(6)] + [("down", j, 0), None]
    return keys


def x_ring_keys():
    keys = []
    for j in range(GT):
        keys += [("qkT", j, f) for f in range(4)]
        if j == 2:
            keys += [("mean", j, 0), ("var", j, 0)]
        keys += [("av", j, 0), ("av", j, 1), ("wo", j, 0)]
    return keys


def build(nc, xT_in, label, wi, wo, swi, swo, g1, g2, wqkv, qk_scale, wout, w1, w2, params,
          rope, mask, ident, out):
    root = ExitStack()
    with root:
        def sem(name):
            return root.enter_context(nc.semaphore(name))

        def sbuf(ctx, name, shape, dt=F32):
            return ctx.enter_context(nc.sbuf_tensor(name, shape, dt))

        psum = root.enter_context(nc.psum_tensor("psum", [P, 8, 512], F32))
        x = sbuf(root, "x", [P, TOK])
        ident_sb = sbuf(root, "ident_sb", [P, P])
        ident_bf = sbuf(root, "ident_bf", [P, P], BF16)
        mask_sb = sbuf(root, "mask_sb", [P, 512])
        mask_bf = sbuf(root, "mask_bf", [P, 512], BF16)
        mean_w = sbuf(root, "mean_w", [P, P])
        base = sbuf(root, "base", [P, 4, HD])
        scl = sbuf(root, "scl", [P, LAYERS, 2, HD])
        par = sbuf(root, "par", [P, LAYERS, NPAR])
        wqkv_sb = sbuf(root, "wqkv_sb", [P, 3 * INNER])
        wout_sb = sbuf(root, "wout_sb", [P, HP, DIM])
        w1_sb = sbuf(root, "w1_sb", [P, 2 * DI])
        w2_sb = sbuf(root, "w2_sb", [P, 3, DIM])

        const_loaded = sem("const_loaded")
        wqkv_loaded, wout_loaded = sem("wqkv_loaded"), sem("wout_loaded")
        w1_loaded = sem("w1_loaded")
        w2_loaded = sem("w2_loaded")

        def load_wqkv(eng, layer):
            return eng.dma_start(wqkv_sb[:, :].unsqueeze(1), wqkv[:, bass.ds(layer, 1), :]).then_inc(wqkv_loaded, 16)

        def load_wout(eng, layer):
            return eng.dma_start(wout_sb[:, :, :].unsqueeze(1), wout[:, bass.ds(layer, 1), :, :]).then_inc(wout_loaded, 16)

        def load_w1(eng, layer):
            eng.dma_start(w1_sb[:, :].unsqueeze(1), w1[:, bass.ds(layer, 1), :]).then_inc(w1_loaded, 16)

        def load_w2(eng, layer):
            eng.dma_start(w2_sb[:, 0:2, :].unsqueeze(1), w2[:, bass.ds(layer, 1), 0:2, :]).then_inc(w2_loaded, 16)
            eng.dma_start(w2_sb[0:85, 2:3, :].unsqueeze(1),
                          w2[0:85, bass.ds(layer, 1), 2:3, :]).then_inc(w2_loaded, 16)

        NE = SHARED + EXPERTS
        NK = NE * EC
        PER = NK // 4
        cond_ctx = ExitStack()
        with cond_ctx as ctx:
            wi_sb = sbuf(ctx, "wi_sb", [P, NE, EF])
            wo_sb = sbuf(ctx, "wo_sb", [P, NE, EC * DIM])
            wi_hi, wi_lo = sbuf(ctx, "wi_hi", [P, NE, EF], F32R), sbuf(ctx, "wi_lo", [P, NE, EF], F32R)
            wo_hi = sbuf(ctx, "wo_hi", [P, NE, EC * DIM], F32R)
            wo_lo = sbuf(ctx, "wo_lo", [P, NE, EC * DIM], F32R)
            g1_sb = sbuf(ctx, "g1_sb", [P, 3, DIM])
            g2_sb = sbuf(ctx, "g2_sb", [P, 3])
            g2_wide = sbuf(ctx, "g2_wide", [P, 3, P])
            lab_i = sbuf(ctx, "lab_i", [P, BATCH], I32)
            lab = sbuf(ctx, "lab", [P, BATCH])
            lab_low = sbuf(ctx, "lab_low", [P, BATCH])
            lab_wrapped = sbuf(ctx, "lab_wrapped", [P, BATCH])
            picked = sbuf(ctx, "picked", [P, EXPERTS, BATCH])
            x_hi, x_lo = sbuf(ctx, "x_hi", [P, GTOK], F32R), sbuf(ctx, "x_lo", [P, GTOK], F32R)
            xm_hi = sbuf(ctx, "xm_hi", [P, 2, GTOK], F32R)
            xm_lo = sbuf(ctx, "xm_lo", [P, 2, GTOK], F32R)
            hid_hi = sbuf(ctx, "hid_hi", [P, 4, GTOK], F32R)
            hid_lo = sbuf(ctx, "hid_lo", [P, 4, GTOK], F32R)
            outs = sbuf(ctx, "outs", [P, 3, GTOK])
            ghid = sbuf(ctx, "ghid", [P, GB])
            logit = sbuf(ctx, "logit", [P, 3, GB])
            gmax = sbuf(ctx, "gmax", [P, GB])
            gdiff = sbuf(ctx, "gdiff", [P, 3, GB])
            gexp = sbuf(ctx, "gexp", [P, 3, GB])
            gsum = sbuf(ctx, "gsum", [P, GB])
            grec = sbuf(ctx, "grec", [P, GB])
            gw = sbuf(ctx, "gw", [P, 3, GB])
            part = sbuf(ctx, "part", [P, 3, GTOK])
            part01 = sbuf(ctx, "part01", [P, GTOK])

            x_loaded, x_rest_loaded = sem("x_loaded"), sem("x_rest_loaded")
            w_loaded = [sem(f"w_loaded{q}") for q in range(NE)]
            small_loaded = sem("small_loaded")
            setup = sem("setup")
            picked_done = sem("picked_done")
            w_hi_done, w_lo_done = sem("w_hi_done"), sem("w_lo_done")
            x_hi_done, x_split = sem("x_hi_done"), sem("x_split")
            xm_ready = sem("xm_ready")
            up_full = [sem(f"up_full{b}") for b in range(4)]
            hid_hi_done = [sem(f"hid_hi_done{b}") for b in range(4)]
            hid_full = [sem(f"hid_full{b}") for b in range(4)]
            hid_used = [sem(f"hid_used{b}") for b in range(4)]
            routed_out, shared_out = sem("routed_out"), sem("shared_out")
            ghid_done, ghid_ready = sem("ghid_done"), sem("ghid_ready")
            logit_done, gdiff_ready, gexp_ready = sem("logit_done"), sem("gdiff_ready"), sem("gexp_ready")
            gate_step = sem("gate_step")
            combined = sem("combined")
            GATE_STEPS = 7
            HID_AT, LOGIT_AT = 4, 8
            OUT_AT, GATE_AT, SPLIT_AT = 16, 12, 24

            def out_of(q):
                return q + 1 if q < SHARED else 0

            with nc.Block() as block:
                @block.sync
                def _(sp):
                    sp.dma_start(x[:, 0:GTOK], xT_in[:, 0:GTOK]).then_inc(x_loaded, 16)
                    for q in range(NE):
                        up, down = (swi[:, q, :], swo[:, q, :, :]) if q < SHARED else (
                            wi[:, q - SHARED, :], wo[:, q - SHARED, :, :])
                        sp.dma_start(wi_sb[:, q, :], up).then_inc(w_loaded[q], 16)
                        sp.dma_start(wo_sb[:, q, :], down.rearrange("p c d -> p (c d)")).then_inc(w_loaded[q], 16)
                        if q == SHARED:
                            sp.dma_start(x[:, GTOK:], xT_in[:, GTOK:]).then_inc(x_rest_loaded, 16)
                    sp.dma_start(ident_sb[:, :], ident).then_inc(const_loaded, 16)
                    sp.dma_start(mask_sb[:, :], mask).then_inc(const_loaded, 16)
                    sp.dma_start(base[:, :, :], rope).then_inc(const_loaded, 16)
                    sp.dma_start(scl[:, :, :, :], qk_scale.unsqueeze(0).to_broadcast(
                        [P, LAYERS, 2, HD])).then_inc(const_loaded, 16)
                    sp.dma_start(par[:, :, :], params).then_inc(const_loaded, 16)
                    load_wqkv(sp, 0)
                    load_wout(sp, 0)
                    load_w1(sp, 0)
                    load_w2(sp, 0)

                @block.gpsimd
                def _(pool):
                    def mask_tokens(g):
                        pool.wait_ge(x_split, g + 1)
                        for e in range(EXPERTS):
                            if e >= 2:
                                pool.wait_ge(up_full[3], g * PER + SHARED + e - 1)
                            else:
                                pool.wait_ge(up_full[3], g * PER)
                            m = picked[:, e, bass.ds(g * GB, GB)].unsqueeze(2).to_broadcast([P, GB, SEQ])
                            for dst, src in ((xm_hi, x_hi), (xm_lo, x_lo)):
                                last = nc.gpsimd.tensor_tensor(
                                    dst[:, e % 2, :].rearrange("p (b s) -> p b s", s=SEQ),
                                    src[:, :].bitcast(F32).rearrange("p (b s) -> p b s", s=SEQ), m, ALU.mult)
                            last.then_inc(xm_ready, 1)

                    pool.wait_ge(picked_done, 1)
                    mask_tokens(0)
                    with pool.Fori(1, GROUPS) as g:
                        mask_tokens(g)

                @block.tensor
                def _(pe):
                    def three(out_ap, w_hi, w_lo, m_hi, m_lo, start, stop):
                        nc.tensor.matmul(out_ap, w_hi, m_hi, start=start, stop=False)
                        nc.tensor.matmul(out_ap, w_hi, m_lo, start=False, stop=False)
                        return nc.tensor.matmul(out_ap, w_lo, m_hi, start=False, stop=stop)

                    def gate_hidden(g):
                        pe.wait_ge(shared_out, (g + 1) * 2)
                        pe.wait_ge(routed_out, g + 1)
                        for c in range(3):
                            first = outs[:, c, :].rearrange("p (b s) -> p b s", s=SEQ)[:, :, 0]
                            last = nc.tensor.matmul(psum[:, 7, 0:GB], g1_sb[:, c, :], first,
                                                    start=c == 0, stop=c == 2)
                        last.then_inc(ghid_done, 1)

                    def gate_logits(g):
                        pe.wait_ge(ghid_ready, g + 1)
                        for c in range(3):
                            last = nc.tensor.matmul(psum[:, 7, GB * (c + 1):GB * (c + 2)], g2_wide[:, c, :],
                                                    ghid[:, :], start=True, stop=True)
                        last.then_inc(logit_done, 1)

                    def experts(g, later):
                        for k in range(NK + 2):
                            if k < NK:
                                q, f, b = k // EC, k % EC, k % 4
                                if k == 0:
                                    pe.wait_ge(x_split, g + 1)
                                if not later and f == 0:
                                    pe.wait_ge(w_lo_done, q + 1)
                                if q >= SHARED and f == 0:
                                    pe.wait_ge(xm_ready, g * EXPERTS + q - SHARED + 1)
                                if later or k >= 4:
                                    pe.wait_ge(hid_full[b], g * PER + k // 4)
                                m_hi, m_lo = (x_hi[:, :], x_lo[:, :]) if q < SHARED else (
                                    xm_hi[:, (q - SHARED) % 2, :], xm_lo[:, (q - SHARED) % 2, :])
                                w = slice(f * P, (f + 1) * P)
                                three(psum[:, b, :], wi_hi[:, q, w], wi_lo[:, q, w], m_hi, m_lo,
                                      True, True).then_inc(up_full[b], 1)
                            if k >= 2:
                                q, f, b = (k - 2) // EC, (k - 2) % EC, (k - 2) % 4
                                if later and k == 2:
                                    pe.wait_ge(shared_out, g * 2)
                                if later and k - 2 == SHARED * EC:
                                    pe.wait_ge(routed_out, g)
                                pe.wait_ge(hid_full[b], g * PER + (k - 2) // 4 + 1)
                                w = slice(f * DIM, (f + 1) * DIM)
                                three(psum[:, 4 + out_of(q), :], wo_hi[:, q, w], wo_lo[:, q, w],
                                      hid_hi[:, b, :], hid_lo[:, b, :], f == 0 and q <= SHARED,
                                      f == EC - 1 and (q < SHARED or q == NE - 1)).then_inc(hid_used[b], 1)
                            if later and k == HID_AT:
                                gate_hidden(g - 1)
                            if later and k == LOGIT_AT:
                                gate_logits(g - 1)

                    pe.wait_ge(small_loaded, 48)
                    pe.wait_ge(setup, 2)
                    experts(0, False)
                    with pe.Fori(1, GROUPS) as g:
                        experts(g, True)
                    gate_hidden(GROUPS - 1)
                    gate_logits(GROUPS - 1)

                @block.scalar
                def _(act):
                    def gate_relu(g):
                        act.wait_ge(ghid_done, g + 1)
                        nc.scalar.activation(ghid[:, :], psum[:, 7, 0:GB], ACT.Relu).then_inc(ghid_ready, 1)

                    def gate_exp(g):
                        act.wait_ge(gdiff_ready, g + 1)
                        nc.scalar.activation(gexp[:, :, :], gdiff[:, :, :], ACT.Exp).then_inc(gexp_ready, 1)

                    def experts(g, later):
                        for k in range(NK):
                            b = k % 4
                            act.wait_ge(up_full[b], g * PER + k // 4 + 1)
                            if later or k >= 4:
                                act.wait_ge(hid_used[b], g * PER + k // 4)
                            nc.scalar.activation(hid_hi[:, b, :], psum[:, b, :], ACT.Relu).then_inc(hid_hi_done[b], 1)
                            if later and k == HID_AT + 1:
                                gate_relu(g - 1)
                            if later and k == GATE_AT:
                                gate_exp(g - 1)
                            if k == OUT_AT:
                                if later:
                                    act.wait_ge(combined, g)
                                act.wait_ge(hid_used[3], g * PER + SHARED)
                                for o in (1, 2):
                                    nc.scalar.copy(outs[:, o, :], psum[:, 4 + o, :]).then_inc(shared_out, 1)

                    act.dma_start(lab_i[:, :], label.unsqueeze(0).to_broadcast([P, BATCH])).then_inc(small_loaded, 16)
                    act.dma_start(g1_sb[:, :, :], g1).then_inc(small_loaded, 16)
                    act.dma_start(g2_sb[:, :], g2).then_inc(small_loaded, 16)
                    for q in range(NE):
                        act.wait_ge(w_loaded[q], 32)
                        nc.scalar.copy(wi_hi[:, q, :], wi_sb[:, q, :]).then_inc(w_hi_done, 1)
                        nc.scalar.copy(wo_hi[:, q, :], wo_sb[:, q, :]).then_inc(w_hi_done, 1)
                    experts(0, False)
                    with act.Fori(1, GROUPS) as g:
                        experts(g, True)
                    gate_relu(GROUPS - 1)
                    gate_exp(GROUPS - 1)

                @block.vector
                def _(dve):
                    n = [0]

                    def prepared(ins):
                        n[0] += 1
                        ins.then_inc(setup, 1)
                        dve.wait_ge(setup, n[0])

                    def split_x(g):
                        if not isinstance(g, int) or g > 0:
                            dve.wait_ge(xm_ready, g * EXPERTS)
                            dve.wait_ge(up_full[3], g * PER - EXPERTS)
                        t = x[:, bass.ds((g & (GROUPS - 1)) * GTOK, GTOK)]
                        nc.vector.tensor_copy(x_hi[:, :], t).then_inc(x_hi_done, 1)
                        dve.wait_ge(x_hi_done, g + 1)
                        nc.vector.tensor_tensor(x_lo[:, :], t, x_hi[:, :].bitcast(F32),
                                                ALU.subtract).then_inc(x_split, 1)

                    def gate(g):
                        steps = [0]

                        def stepped(ins):
                            steps[0] += 1
                            ins.then_inc(gate_step, 1)
                            dve.wait_ge(gate_step, g * GATE_STEPS + steps[0])

                        wide = "p (b s) -> p b s"
                        dve.wait_ge(logit_done, g + 1)
                        stepped(nc.vector.tensor_copy(logit[:, :, :], psum[:, 7, GB:4 * GB].rearrange(
                            "p (o b) -> p o b", b=GB)))
                        stepped(nc.vector.tensor_reduce(gmax[:, :], logit[:, :, :].rearrange("p o b -> p b o"),
                                                        AX_X, ALU.max))
                        nc.vector.tensor_tensor(gdiff[:, :, :], logit[:, :, :],
                                                gmax[:, :].unsqueeze(1).to_broadcast([P, 3, GB]),
                                                ALU.subtract).then_inc(gdiff_ready, 1)
                        dve.wait_ge(gexp_ready, g + 1)
                        stepped(nc.vector.tensor_reduce(gsum[:, :], gexp[:, :, :].rearrange("p o b -> p b o"),
                                                        AX_X, ALU.add))
                        stepped(nc.vector.reciprocal(grec[:, :], gsum[:, :]))
                        stepped(nc.vector.tensor_tensor(gw[:, :, :], gexp[:, :, :],
                                                        grec[:, :].unsqueeze(1).to_broadcast([P, 3, GB]), ALU.mult))
                        dve.wait_ge(shared_out, (g + 1) * 2)
                        for o in range(3):
                            last = nc.vector.tensor_tensor(
                                part[:, o, :].rearrange(wide, s=SEQ), outs[:, o, :].rearrange(wide, s=SEQ),
                                gw[:, o, :].unsqueeze(2).to_broadcast([P, GB, SEQ]), ALU.mult)
                        stepped(last)
                        stepped(nc.vector.tensor_tensor(part01[:, :], part[:, 0, :], part[:, 1, :], ALU.add))
                        nc.vector.tensor_tensor(x[:, bass.ds(g * GTOK, GTOK)], part01[:, :],
                                                part[:, 2, :], ALU.add).then_inc(combined, 1)
                        assert steps[0] == GATE_STEPS

                    def experts(g, later):
                        for k in range(NK):
                            b = k % 4
                            dve.wait_ge(hid_hi_done[b], g * PER + k // 4 + 1)
                            nc.vector.scalar_tensor_tensor(hid_lo[:, b, :], psum[:, b, :], 0.0,
                                                           hid_hi[:, b, :].bitcast(F32), ALU.max,
                                                           ALU.subtract).then_inc(hid_full[b], 1)
                            if later and k == GATE_AT:
                                gate(g - 1)
                            if k == SPLIT_AT:
                                split_x(g + 1)
                        for b in range(4):
                            dve.wait_ge(hid_used[b], (g + 1) * PER)
                        nc.vector.tensor_copy(outs[:, 0, :], psum[:, 4, :]).then_inc(routed_out, 1)

                    prepared(nc.vector.memset(mean_w[:, :], 1.0 / DIM))
                    dve.wait_ge(small_loaded, 48)
                    prepared(nc.vector.tensor_copy(g2_wide[:, :, :], g2_sb[:, :].unsqueeze(2).to_broadcast([P, 3, P])))
                    prepared(nc.vector.tensor_copy(lab[:, :], lab_i[:, :]))
                    prepared(nc.vector.tensor_scalar(lab_low[:, :], lab[:, :], 0.0, float(EXPERTS), ALU.is_lt, ALU.mult))
                    prepared(nc.vector.tensor_tensor(lab_wrapped[:, :], lab[:, :], lab_low[:, :], ALU.add))
                    prepared(nc.vector.tensor_scalar(lab[:, :], lab_wrapped[:, :], 0.0, float(EXPERTS - 1), ALU.max, ALU.min))
                    for e in range(EXPERTS):
                        last = nc.vector.tensor_scalar(picked[:, e, :], lab[:, :], float(e), None, ALU.is_equal)
                    last.then_inc(picked_done, 1)
                    dve.wait_ge(x_loaded, 16)
                    split_x(0)
                    for q in range(NE):
                        dve.wait_ge(w_hi_done, 2 * q + 2)
                        nc.vector.tensor_tensor(wi_lo[:, q, :], wi_sb[:, q, :], wi_hi[:, q, :].bitcast(F32), ALU.subtract)
                        nc.vector.tensor_tensor(wo_lo[:, q, :], wo_sb[:, q, :], wo_hi[:, q, :].bitcast(F32),
                                                ALU.subtract).then_inc(w_lo_done, 1)
                    dve.wait_ge(x_rest_loaded, 16)
                    experts(0, False)
                    with dve.Fori(1, GROUPS) as g:
                        experts(g, True)
                    gate(GROUPS - 1)
                    dve.wait_ge(const_loaded, 80)
                    prepared(nc.vector.tensor_copy(ident_bf[:, :], ident_sb[:, :]))
                    prepared(nc.vector.tensor_copy(mask_bf[:, :], mask_sb[:, :]))

        layers_ctx = ExitStack()
        ctx = layers_ctx
        xs_hi = sbuf(ctx, "xs_hi", [P, 2, TILE], F32R)
        xs_lo = sbuf(ctx, "xs_lo", [P, 2, TILE], F32R)
        wqkv_hi = sbuf(ctx, "wqkv_hi", [P, 3 * INNER], F32R)
        wqkv_lo = sbuf(ctx, "wqkv_lo", [P, 3 * INNER], F32R)
        w1_hi = sbuf(ctx, "w1_hi", [P, 2 * DI], F32R)
        w1_lo = sbuf(ctx, "w1_lo", [P, 2 * DI], F32R)
        tab = sbuf(ctx, "tab", [P, 4, HD])
        lp = sbuf(ctx, "lp", [P, NPAR])
        sq = sbuf(ctx, "sq", [P, 4, 512])
        rcos = sbuf(ctx, "rcos", [P, 2, 4, 512])
        rsin = sbuf(ctx, "rsin", [P, 4, 512])
        ss = sbuf(ctx, "ss", [P, 2, 2 * HEADS])
        ssc = sbuf(ctx, "ssc", [P, 2, 2 * HEADS])
        lns = sbuf(ctx, "lns", [P, 2 * HEADS])
        y0 = sbuf(ctx, "y0", [P, 2, 2 * HEADS])
        nt_a = sbuf(ctx, "nt_a", [P, 2 * HEADS])
        nt_b = sbuf(ctx, "nt_b", [P, 2 * HEADS])
        rn = sbuf(ctx, "rn", [P, 2, 2 * HEADS])
        v_sb = sbuf(ctx, "v_sb", [P, 4, INNER])
        qT = sbuf(ctx, "qT", [P, HP, TILE])
        kbd = sbuf(ctx, "kbd", [P, HP, 2, TILE + SEQ])
        mx = sbuf(ctx, "mx", [P, HEADS])
        s_sb = sbuf(ctx, "s_sb", [P, HEADS, SEQ])
        p_sb = sbuf(ctx, "p_sb", [P, HEADS, SEQ])
        sums = sbuf(ctx, "sums", [P, HEADS])
        rinv = sbuf(ctx, "rinv", [P, HEADS])
        pT = sbuf(ctx, "pT", [P, HEADS, SEQ])
        bd = sbuf(ctx, "bd", [P, HEADS, TILE])
        oT = sbuf(ctx, "oT", [P, HP, TILE])
        xs2 = sbuf(ctx, "xs2", [P, GTOK])
        xc = sbuf(ctx, "xc", [P, GTOK])
        xsq = sbuf(ctx, "xsq", [P, GTOK])
        lnv = sbuf(ctx, "lnv", [P, GTOK])
        rstd = sbuf(ctx, "rstd", [P, GTOK])
        xg = sbuf(ctx, "xg", [P, GTOK])
        xn_hi = sbuf(ctx, "xn_hi", [P, GTOK], F32R)
        xn_lo = sbuf(ctx, "xn_lo", [P, GTOK], F32R)
        gel = sbuf(ctx, "gel", [P, 3, GTOK])
        h = sbuf(ctx, "h", [P, 3, GTOK])
        eps = sbuf(ctx, "eps", [P, 1])

        a_ring, x_ring = Ring(4, a_ring_keys()), Ring(2, x_ring_keys())
        a_full, a_free = [sem(f"a_full{b}") for b in range(4)], [sem(f"a_free{b}") for b in range(4)]
        x_full, x_free = [sem(f"x_full{b}") for b in range(2)], [sem(f"x_free{b}") for b in range(2)]
        X0, S0 = 4, 6

        zeroed = sem("zeroed")
        wqkv_hi_done, wqkv_lo_done = sem("wqkv_hi_done"), sem("wqkv_lo_done")
        w1_hi_done, w1_lo_done = sem("w1_hi_done"), sem("w1_lo_done")
        xs_hi_done = sem("xs_hi_done")
        xs_ready = sem("xs_ready")
        sq_done = sem("sq_done")
        sums_done = sem("sums_done")
        y0_done = sem("y0_done")
        rn_done = sem("rn_done")
        qadd_done, kadd_done = sem("qadd_done"), sem("kadd_done")
        k_ready = sem("k_ready")
        scores_done = sem("scores_done")
        s_done = sem("s_done")
        smul_done = sem("smul_done")
        exp_done = sem("exp_done")
        rinv_done = sem("rinv_done")
        pn_done = sem("pn_done")
        pT_done = sem("pT_done")
        bd_done = sem("bd_done")
        res_done = sem("res_done")
        dve_norm = sem("dve_norm")
        dve_soft = sem("dve_soft")
        act_norm = sem("act_norm")
        tab_done = sem("tab_done")
        xs2_done = sem("xs2_done")
        xsq_done = sem("xsq_done")
        act_var = sem("act_var")
        rstd_done = sem("rstd_done")
        xg_done, xn_hi_done, xn_done = sem("xg_done"), sem("xn_hi_done"), sem("xn_done")

        with nc.Block() as block:
            @block.sync
            def _(sp):
                with sp.Fori(1, LAYERS) as layer:
                    last = layer * GROUPS - 1
                    sp.wait_ge(wqkv_lo_done, layer * 6)
                    load_wqkv(sp, layer)
                    sp.wait_ge(w1_lo_done, layer)
                    load_w1(sp, layer)
                    sp.wait_ge(x_full[x_ring.bank(("wo", 1, 0))], x_ring.nth(("wo", 1, 0), last + 1))
                    load_wout(sp, layer)
                    sp.wait_ge(a_full[a_ring.bank(("down", 3, 0))], a_ring.nth(("down", 3, 0), last + 1))
                    load_w2(sp, layer)

            @block.tensor
            def _(pe):
                def project(it, j, c):
                    n = it * GT + j
                    if c == 0:
                        pe.wait_ge(xs_ready, n + 1)
                    if j == 0:
                        pe.wait_ge(wqkv_lo_done, (it >> 3) * 6 + c + 1)
                    b = a_ring.bank(("qkv", j, c))
                    w = slice(c * 512, (c + 1) * 512)
                    pe.wait_ge(a_free[b], a_ring.nth(("qkv", j, c), it) - 1)
                    nc.tensor.matmul(psum[:, b, :], xs_hi[:, j % 2, :], wqkv_hi[:, w], start=True, stop=False)
                    nc.tensor.matmul(psum[:, b, :], xs_hi[:, j % 2, :], wqkv_lo[:, w], start=False, stop=False)
                    nc.tensor.matmul(psum[:, b, :], xs_lo[:, j % 2, :], wqkv_hi[:, w],
                                     start=False, stop=True).then_inc(a_full[b], 1)

                def transpose_qk(it, j, f):
                    m = it * GT + j - 1
                    if f == 0:
                        pe.wait_ge(qadd_done, m + 1)
                    if f == 2:
                        pe.wait_ge(k_ready, m + 1)
                    b = x_ring.bank(("qkT", j, f))
                    pe.wait_ge(x_free[b], x_ring.nth(("qkT", j, f), it) - 1)
                    for i in range(4):
                        last = nc.tensor.transpose(psum[:, X0 + b, i * P:(i + 1) * P],
                                                   rcos[:, (j - 1) % 2, f, i * P:(i + 1) * P], ident_sb[:, :])
                    last.then_inc(x_full[b], 1)

                def score(it, j):
                    m = it * GT + j - 1
                    pe.wait_ge(s_done, known(m))
                    pe.wait_ge(x_free[x_ring.bank(("qkT", j, 2))], x_ring.nth(("qkT", j, 2), it))
                    pe.wait_ge(x_free[x_ring.bank(("qkT", j, 3))], x_ring.nth(("qkT", j, 3), it))
                    for o in range(2):
                        nc.tensor.matmul(psum[:, S0 + o, :], ident_bf[:, :], mask_bf[:, :],
                                         start=True, stop=False, skip_group_check=True)
                    for hp in range(HP):
                        for b in range(TB):
                            col = (hp % 4) * P
                            last = nc.tensor.matmul(
                                psum[SEQ * b:SEQ * (b + 1), S0 + hp // 4, col:col + P],
                                qT[:, hp, SEQ * b:SEQ * (b + 1)], kbd[:, hp, :, SEQ * b:SEQ * (b + 2)],
                                start=False, stop=True, skip_group_check=True)
                    last.then_inc(scores_done, 1)

                def attend(it, j):
                    m = it * GT + j - 2
                    pe.wait_ge(bd_done, known(m + 1))
                    for f in range(2):
                        b = x_ring.bank(("av", j, f))
                        pe.wait_ge(x_free[b], x_ring.nth(("av", j, f), it) - 1)
                        pe.wait_ge(const_loaded, 80)
                        for i in range(4):
                            for odd in range(2):
                                hh = 2 * (4 * f + i) + odd
                                last = nc.tensor.matmul(
                                    psum[64 * odd:64 * odd + 64, X0 + b, i * P:(i + 1) * P],
                                    v_sb[:, (j - 2) % 4, hh * HD:(hh + 1) * HD], bd[:, hh, :],
                                    start=True, stop=True)
                        last.then_inc(x_full[b], 1)

                def project_out(it, j):
                    if j in (0, 2):
                        pe.wait_ge(wout_loaded, known((((it * GT + j - 2) >> 5) + 1) * 16))
                    b = x_ring.bank(("wo", j, 0))
                    pe.wait_ge(x_free[b], x_ring.nth(("wo", j, 0), it) - 1)
                    for hp in range(HP):
                        if hp % 4 == 0:
                            key = ("av", j, hp // 4)
                            pe.wait_ge(x_free[x_ring.bank(key)], x_ring.nth(key, it))
                        last = nc.tensor.matmul(psum[:, X0 + b, 0:TILE], wout_sb[:, hp, :], oT[:, hp, :],
                                                start=hp == 0, stop=hp == HP - 1)
                    last.then_inc(x_full[b], 1)

                def mean(it, key, src, ready):
                    pe.wait_ge(ready, known(it))
                    b = x_ring.bank(key)
                    pe.wait_ge(x_free[b], x_ring.nth(key, it) - 1)
                    nc.tensor.matmul(psum[:, X0 + b, :], mean_w[:, :], src[:, :], start=True,
                                     stop=True).then_inc(x_full[b], 1)

                def ffn_up(it, j):
                    pe.wait_ge(xn_done, it)
                    pe.wait_ge(w1_lo_done, ((it - 1) >> 3) + 1)
                    for c in range(6):
                        off, w = FC[c % 3]
                        off += DI if c < 3 else 0
                        b = a_ring.bank(("up", j, c))
                        pe.wait_ge(a_free[b], a_ring.nth(("up", j, c), it) - 1)
                        nc.tensor.matmul(psum[0:w, b, :], w1_hi[:, off:off + w], xn_hi[:, :], start=True, stop=False)
                        nc.tensor.matmul(psum[0:w, b, :], w1_hi[:, off:off + w], xn_lo[:, :], start=False, stop=False)
                        nc.tensor.matmul(psum[0:w, b, :], w1_lo[:, off:off + w], xn_hi[:, :], start=False,
                                         stop=True).then_inc(a_full[b], 1)

                def ffn_down(it, j):
                    pe.wait_ge(w2_loaded, (((it - 1) >> 3) + 1) * 32)
                    b = a_ring.bank(("down", j, 0))
                    pe.wait_ge(a_free[b], a_ring.nth(("down", j, 0), it) - 1)
                    for c in (3, 4, 5):
                        pe.wait_ge(a_free[a_ring.bank(("up", j, c))], a_ring.nth(("up", j, c), it))
                    for c in range(3):
                        w = FC[c][1]
                        last = nc.tensor.matmul(psum[:, b, :], w2_sb[0:w, c, :], h[0:w, c, :],
                                                start=c == 0, stop=c == 2)
                    last.then_inc(a_full[b], 1)

                def turn(it):
                    for j in range(GT):
                        for c in range(6):
                            if has_front(it):
                                project(it, j, c)
                            if c < 4 and has_cd(it, j):
                                transpose_qk(it, j, c)
                        if j == 2 and has_ffn(it):
                            mean(it, ("mean", j, 0), xs2, xs2_done)
                        if j == 3 and has_ffn(it):
                            ffn_up(it, j)
                        if has_cd(it, j):
                            score(it, j)
                        if j == 2 and has_ffn(it):
                            mean(it, ("var", j, 0), xsq, xsq_done)
                        if has_ef(it, j):
                            attend(it, j)
                            project_out(it, j)
                        if j == 3 and has_ffn(it):
                            ffn_down(it, j)

                pe.wait_ge(zeroed, 1)
                turn(0)
                with pe.Fori(1, TURNS) as it:
                    turn(it)
                turn(TURNS)

            @block.scalar
            def _(act):
                def split_wqkv(it, c):
                    act.wait_ge(wqkv_loaded, ((it >> 3) + 1) * 16)
                    if not isinstance(it, int):
                        key = ("qkv", 3, 5)
                        act.wait_ge(a_full[a_ring.bank(key)], a_ring.nth(key, it - 1))
                    w = slice(c * 512, (c + 1) * 512)
                    nc.scalar.copy(wqkv_hi[:, w], wqkv_sb[:, w]).then_inc(wqkv_hi_done, 1)

                def split_w1(it):
                    layer = it >> 3
                    act.wait_ge(w1_loaded, (layer + 1) * 16)
                    if not isinstance(it, int):
                        key = ("up", 3, 5)
                        act.wait_ge(a_full[a_ring.bank(key)], a_ring.nth(key, it))
                    nc.scalar.copy(w1_hi[:, :], w1_sb[:, :]).then_inc(w1_hi_done, 1)

                def square(it, j, c):
                    n = it * GT + j
                    if c == 0:
                        act.wait_ge(sums_done, known(n))
                    b = a_ring.bank(("qkv", j, c))
                    act.wait_ge(a_full[b], a_ring.nth(("qkv", j, c), it))
                    nc.scalar.activation(sq[:, c, :], psum[:, b, :], ACT.Square).then_inc(sq_done, 1)

                def block_diagonal(it, j):
                    m = it * GT + j - 2
                    act.wait_ge(pT_done, known(m + 1))
                    for b in range(TB):
                        t = slice(SEQ * b, SEQ * b + SEQ)
                        last = nc.scalar.copy(bd[t, :, t], pT[t, :, :])
                    last.then_inc(bd_done, 1)

                def values(it, j):
                    for c in (4, 5):
                        b = a_ring.bank(("qkv", j, c))
                        act.wait_ge(a_full[b], a_ring.nth(("qkv", j, c), it))
                        nc.scalar.copy(v_sb[:, j, (c - 4) * 512:(c - 3) * 512],
                                       psum[:, b, :]).then_inc(a_free[b], 1)

                def take_qkT(it, j, f):
                    m = it * GT + j - 1
                    if f == 0:
                        act.wait_ge(scores_done, known(m))
                    b = x_ring.bank(("qkT", j, f))
                    pairs = slice(4 * (f % 2), 4 * (f % 2) + 4)
                    act.wait_ge(x_full[b], x_ring.nth(("qkT", j, f), it))
                    src = psum[:, X0 + b, :].rearrange("p (i t) -> p i t", t=TILE)
                    if f < 2:
                        nc.scalar.copy(qT[:, pairs, :], src).then_inc(x_free[b], 1)
                    else:
                        nc.scalar.copy(kbd[0:64, pairs, 0, 0:TILE], src[0:64, :, :])
                        nc.scalar.copy(kbd[64:128, pairs, 1, 0:TILE], src[64:128, :, :]).then_inc(x_free[b], 1)

                def guess_norms(it, j):
                    n = it * GT + j
                    act.wait_ge(sums_done, known(n + 1))
                    nc.scalar.activation(lns[:, :], ssc[:, j % 2, :], ACT.Ln, scale=SS_SCALE).then_inc(act_norm, 1)
                    act.wait_ge(act_norm, known(n + 1))
                    nc.scalar.activation(y0[:, j % 2, :], lns[:, :], ACT.Exp, scale=-0.5).then_inc(y0_done, 1)

                def take_oT(it, j):
                    for f in range(2):
                        b = x_ring.bank(("av", j, f))
                        act.wait_ge(x_full[b], x_ring.nth(("av", j, f), it))
                        nc.scalar.copy(oT[:, 4 * f:4 * f + 4, :], psum[:, X0 + b, :].rearrange(
                            "p (i t) -> p i t", t=TILE)).then_inc(x_free[b], 1)

                def exponentials(it, j):
                    m = it * GT + j - 1
                    act.wait_ge(smul_done, known(m + 1))
                    nc.scalar.activation(p_sb[:, :, :], s_sb[:, :, :], ACT.Exp).then_inc(exp_done, 1)

                def turn(it):
                    for j in range(GT):
                        if j == 0 and has_front(it):
                            with first_turn_of_layer(act, it):
                                for c in range(6):
                                    split_wqkv(it, c)
                        for c in range(4):
                            if has_front(it):
                                square(it, j, c)
                            if has_cd(it, j):
                                take_qkT(it, j, c)
                        if has_ef(it, j):
                            block_diagonal(it, j)
                        if has_front(it):
                            values(it, j)
                        if j == 3 and has_ffn(it):
                            for c in range(3):
                                w = FC[c][1]
                                b = a_ring.bank(("up", j, c))
                                act.wait_ge(a_full[b], a_ring.nth(("up", j, c), it))
                                nc.scalar.activation(gel[0:w, c, :], psum[0:w, b, :], ACT.Gelu,
                                                     bias=lp[0:w, PBG + c:PBG + c + 1]
                                                     ).then_inc(a_free[b], 1)
                            nc.scalar.preload_act_table_set(LN_EXP_SET)
                        if j == 2 and has_ffn(it):
                            act.wait_ge(x_free[x_ring.bank(("mean", j, 0))], x_ring.nth(("mean", j, 0), it))
                            nc.scalar.activation(xsq[:, :], xc[:, :], ACT.Square).then_inc(xsq_done, 1)
                        if has_front(it):
                            guess_norms(it, j)
                        if j == 2 and has_ffn(it):
                            b = x_ring.bank(("var", j, 0))
                            act.wait_ge(x_full[b], x_ring.nth(("var", j, 0), it))
                            nc.scalar.activation(lnv[:, :], psum[:, X0 + b, :], ACT.Ln,
                                                 bias=eps[:, :]).then_inc(x_free[b], 1)
                            act.wait_ge(x_free[x_ring.bank(("var", j, 0))], x_ring.nth(("var", j, 0), it))
                            nc.scalar.activation(rstd[:, :], lnv[:, :], ACT.Exp, scale=-0.5).then_inc(rstd_done, 1)
                        if has_ef(it, j):
                            take_oT(it, j)
                        if has_cd(it, j):
                            exponentials(it, j)
                        if j == 3 and has_front(it):
                            with first_turn_of_layer(act, it):
                                split_w1(it)

                nc.scalar.preload_act_table_set(LN_EXP_SET)
                act.wait_ge(zeroed, 1)
                turn(0)
                with act.Fori(1, TURNS) as it:
                    turn(it)
                turn(TURNS)

            @block.gpsimd
            def _(pool):
                def swapped_add(it, j, qk):
                    for half in range(2):
                        own = slice(half * 32, half * 32 + 32)
                        other = slice(32 - half * 32, 64 - half * 32)
                        c = rcos[:, j % 2, 2 * qk:2 * qk + 2, :].rearrange("p c (h e) -> p (c h) e", e=HD)
                        s = rsin[:, 2 * qk:2 * qk + 2, :].rearrange("p c (h e) -> p (c h) e", e=HD)
                        last = nc.gpsimd.tensor_tensor(c[:, :, own], c[:, :, own], s[:, :, other], ALU.add)
                    return last

                def turn(it):
                    for j in range(GT):
                        n = it * GT + j
                        if has_front(it):
                            pool.wait_ge(a_free[a_ring.bank(("qkv", j, 0))], a_ring.nth(("qkv", j, 0), it))
                            pool.wait_ge(a_free[a_ring.bank(("qkv", j, 1))], a_ring.nth(("qkv", j, 1), it))
                            swapped_add(it, j, 0).then_inc(qadd_done, 1)
                            pool.wait_ge(a_free[a_ring.bank(("qkv", j, 2))], a_ring.nth(("qkv", j, 2), it))
                            pool.wait_ge(a_free[a_ring.bank(("qkv", j, 3))], a_ring.nth(("qkv", j, 3), it))
                            swapped_add(it, j, 1).then_inc(kadd_done, 1)
                        if has_cd(it, j):
                            pool.wait_ge(s_done, known(n))
                            pool.wait_ge(rn_done, known(n))
                            nc.gpsimd.tensor_tensor(s_sb[:, :, :], s_sb[:, :, :],
                                                    rn[:, (j - 1) % 2, 0:HEADS].unsqueeze(2).to_broadcast(
                                                        [P, HEADS, SEQ]),
                                                    ALU.mult).then_inc(smul_done, 1)
                        if has_front(it):
                            pool.wait_ge(rn_done, known(n + 1))
                            pool.wait_ge(kadd_done, known(n + 1))
                            k = rcos[:, j % 2, 2:4, :].rearrange("p c (h e) -> p (c h) e", e=HD)
                            nc.gpsimd.tensor_tensor(k, k, rn[:, j % 2, HEADS:].unsqueeze(2).to_broadcast(
                                [P, HEADS, HD]), ALU.mult).then_inc(k_ready, 1)
                        if has_cd(it, j):
                            pool.wait_ge(rinv_done, known(n))
                            nc.gpsimd.tensor_tensor(p_sb[:, :, :], p_sb[:, :, :],
                                                    rinv[:, :].unsqueeze(2).to_broadcast([P, HEADS, SEQ]),
                                                    ALU.mult).then_inc(pn_done, 1)

                turn(0)
                with pool.Fori(1, TURNS) as it:
                    turn(it)
                turn(TURNS)

            @block.vector
            def _(dve):
                def shift(dst, src, cols):
                    nc.vector.tensor_copy(dst[0:64, :], src[0:64, :])
                    return nc.vector.tensor_copy(
                        dst[64:128, :].rearrange("p (b s) -> p b s", s=SEQ)[:, :, 1:SEQ],
                        src[64:128, :].rearrange("p (b s) -> p b s", s=SEQ)[:, :, 0:SEQ - 1])

                def shift_split(buf, src, n):
                    lower, upper = slice(0, 64), slice(64, 128)
                    to, of = (lambda t: t.rearrange("p (b s) -> p b s", s=SEQ)[:, :, 1:SEQ],
                              lambda t: t.rearrange("p (b s) -> p b s", s=SEQ)[:, :, 0:SEQ - 1])
                    hi, lo = xs_hi[:, buf, :], xs_lo[:, buf, :]
                    nc.vector.tensor_copy(hi[lower, :], src[lower, :])
                    nc.vector.tensor_copy(to(hi[upper, :]), of(src[upper, :])).then_inc(xs_hi_done, 1)
                    dve.wait_ge(xs_hi_done, n + 1)
                    nc.vector.tensor_tensor(lo[lower, :], src[lower, :], hi[lower, :].bitcast(F32), ALU.subtract)
                    nc.vector.tensor_tensor(to(lo[upper, :]), of(src[upper, :]), to(hi[upper, :].bitcast(F32)),
                                            ALU.subtract).then_inc(xs_ready, 1)

                def split_wqkv(it):
                    for c in range(6):
                        w = slice(c * 512, (c + 1) * 512)
                        dve.wait_ge(wqkv_hi_done, (it >> 3) * 6 + c + 1)
                        nc.vector.tensor_tensor(wqkv_lo[:, w], wqkv_sb[:, w], wqkv_hi[:, w].bitcast(F32),
                                                ALU.subtract).then_inc(wqkv_lo_done, 1)

                def split_w1(it):
                    dve.wait_ge(w1_hi_done, (it >> 3) + 1)
                    nc.vector.tensor_tensor(w1_lo[:, :], w1_sb[:, :], w1_hi[:, :].bitcast(F32),
                                            ALU.subtract).then_inc(w1_lo_done, 1)

                def tile_of(n):
                    return x[:, bass.ds((n & (TOK // TILE - 1)) * TILE, TILE)]

                def group_of(it):
                    return x[:, bass.ds(((it - 1) & (GROUPS - 1)) * GTOK, GTOK)]

                def tables(it):
                    layer = layer_of(it)
                    for qk in range(2):
                        s = scl[:, bass.ds(layer, 1), qk, :]
                        last = nc.vector.tensor_tensor(tab[:, 2 * qk:2 * qk + 2, :], base[:, 2 * qk:2 * qk + 2, :],
                                                       s.to_broadcast([P, 2, HD]), ALU.mult)
                    last.then_inc(tab_done, 1)
                    dve.wait_ge(tab_done, known(it + 1))

                def transpose_p(it, j):
                    m = it * GT + j - 2
                    dve.wait_ge(pn_done, known(m + 1))
                    dve.wait_ge(bd_done, known(m))
                    nc.vector.transpose(pT[:, :, :], p_sb[:, :, :]).then_inc(pT_done, 1)

                def rotary(it, j):
                    n = it * GT + j
                    dve.wait_ge(kadd_done, known(n))
                    for c in range(4):
                        b = a_ring.bank(("qkv", j, c))
                        dve.wait_ge(sq_done, known(n * 4 + c + 1))
                        src = psum[:, b, :].rearrange("p (h e) -> p h e", e=HD)
                        for dst, t in ((rcos[:, j % 2, c, :], 2 * (c // 2)), (rsin[:, c, :], 2 * (c // 2) + 1)):
                            last = nc.vector.tensor_tensor(
                                dst.rearrange("p (h e) -> p h e", e=HD), src,
                                tab[:, t:t + 1, :].to_broadcast([P, 8, HD]), ALU.mult)
                        last.then_inc(a_free[b], 1)

                def sum_squares(it, j):
                    n = it * GT + j
                    nc.vector.tensor_reduce(ss[:, j % 2, :], sq[:, :, :].rearrange("p c (h e) -> p (c h) e", e=HD),
                                            AX_X, ALU.add).then_inc(dve_norm, 1)
                    dve.wait_ge(dve_norm, known(n * 3 + 1))
                    nc.vector.tensor_scalar(ssc[:, j % 2, :], ss[:, j % 2, :], 1e-24, None,
                                            ALU.max).then_inc(sums_done, 1)

                def refine_norms(it, j):
                    n = it * GT + j
                    dve.wait_ge(y0_done, known(n + 1))
                    nc.vector.scalar_tensor_tensor(nt_a[:, :], y0[:, j % 2, :], Y_SCALE * Y_SCALE, y0[:, j % 2, :],
                                                   ALU.mult, ALU.mult).then_inc(dve_norm, 1)
                    dve.wait_ge(dve_norm, known(n * 3 + 2))
                    nc.vector.scalar_tensor_tensor(nt_b[:, :], nt_a[:, :], -0.5 * Y_SCALE, ssc[:, j % 2, :],
                                                   ALU.mult, ALU.mult).then_inc(dve_norm, 1)
                    dve.wait_ge(dve_norm, known(n * 3 + 3))
                    nc.vector.scalar_tensor_tensor(rn[:, j % 2, :], nt_b[:, :], 1.5 * Y_SCALE, y0[:, j % 2, :],
                                                   ALU.add, ALU.mult).then_inc(rn_done, 1)

                def subtract_max(it, j):
                    m = it * GT + j - 1
                    s = psum[:, S0:S0 + 2, :].rearrange("p o (h w) -> p (o h) w", w=2 * SEQ)[:, :, 0:SEQ]
                    dve.wait_ge(scores_done, known(m + 1))
                    nc.vector.tensor_reduce(mx[:, :], s, AX_X, ALU.max).then_inc(dve_soft, 1)
                    dve.wait_ge(dve_soft, known(m * 2 + 1))
                    nc.vector.tensor_tensor(s_sb[:, :, :], s, mx[:, :].unsqueeze(2).to_broadcast(
                        [P, HEADS, SEQ]), ALU.subtract).then_inc(s_done, 1)

                def sum_exp(it, j):
                    m = it * GT + j - 1
                    dve.wait_ge(exp_done, known(m + 1))
                    nc.vector.tensor_reduce(sums[:, :], p_sb[:, :, :], AX_X, ALU.add).then_inc(dve_soft, 1)
                    dve.wait_ge(dve_soft, known(m * 2 + 2))
                    nc.vector.reciprocal(rinv[:, :], sums[:, :]).then_inc(rinv_done, 1)

                def add_attention(it, j):
                    m = it * GT + j - 2
                    b = x_ring.bank(("wo", j, 0))
                    dve.wait_ge(x_full[b], x_ring.nth(("wo", j, 0), it))
                    t = tile_of(m)
                    nc.vector.tensor_tensor(t, psum[:, X0 + b, 0:TILE], t, ALU.add).then_inc(x_free[b], 1)

                def turn(it):
                    for j in range(GT):
                        n = it * GT + j
                        if j == 0 and has_front(it):
                            with first_turn_of_layer(dve, it):
                                split_wqkv(it)
                            tables(it)
                        if has_ef(it, j):
                            transpose_p(it, j)
                        if has_front(it):
                            rotary(it, j)
                            sum_squares(it, j)
                            b = a_ring.bank(("qkv", j, 0))
                            dve.wait_ge(a_full[b], a_ring.nth(("qkv", j, 0), it))
                            if not (isinstance(it, int) and it == 0):
                                dve.wait_ge(a_free[a_ring.bank(("down", 3, 0))], a_ring.nth(("down", 3, 0), it - 1))
                            shift_split((j + 1) % 2, tile_of(n + 1), n + 1)
                        if j == 2 and has_ffn(it):
                            b = x_ring.bank(("mean", j, 0))
                            dve.wait_ge(x_full[b], x_ring.nth(("mean", j, 0), it))
                            nc.vector.tensor_tensor(xc[:, :], xs2[:, :], psum[:, X0 + b, :],
                                                    ALU.subtract).then_inc(x_free[b], 1)
                        if j == 3 and has_ffn(it):
                            for c in range(3):
                                w = FC[c][1]
                                dve.wait_ge(a_free[a_ring.bank(("up", j, c))], a_ring.nth(("up", j, c), it))
                                b = a_ring.bank(("up", j, 3 + c))
                                dve.wait_ge(a_full[b], a_ring.nth(("up", j, 3 + c), it))
                                nc.vector.scalar_tensor_tensor(h[0:w, c, :], psum[0:w, b, :],
                                                               lp[0:w, PBA + c:PBA + c + 1], gel[0:w, c, :],
                                                               ALU.add, ALU.mult).then_inc(a_free[b], 1)
                        if has_front(it):
                            refine_norms(it, j)
                        if has_cd(it, j):
                            subtract_max(it, j)
                            sum_exp(it, j)
                        if has_ef(it, j):
                            add_attention(it, j)
                        if j == 1 and has_ffn(it):
                            dve.wait_ge(x_free[x_ring.bank(("wo", 1, 0))], x_ring.nth(("wo", 1, 0), it))
                            dve.wait_ge(x_free[x_ring.bank(("wo", 0, 0))], x_ring.nth(("wo", 0, 0), it))
                            layer = layer_of(it - 1)
                            nc.vector.tensor_copy(
                                lp[:, :].unsqueeze(1),
                                par[:, bass.ds(layer, 1), :])
                            shift(xs2[:, :], group_of(it), GTOK).then_inc(xs2_done, 1)
                        if j == 2 and has_ffn(it):
                            dve.wait_ge(rstd_done, known(it))
                            nc.vector.scalar_tensor_tensor(xg[:, :], xc[:, :], lp[:, PG:PG + 1], rstd[:, :],
                                                           ALU.mult, ALU.mult).then_inc(xg_done, 1)
                            dve.wait_ge(xg_done, known(it))
                            nc.vector.tensor_scalar(xn_hi[:, :], xg[:, :], lp[:, PB:PB + 1], None,
                                                    ALU.add).then_inc(xn_hi_done, 1)
                            dve.wait_ge(xn_hi_done, it)
                            nc.vector.scalar_tensor_tensor(xn_lo[:, :], xg[:, :], lp[:, PB:PB + 1],
                                                           xn_hi[:, :].bitcast(F32), ALU.add,
                                                           ALU.subtract).then_inc(xn_done, 1)
                        if j == 3 and has_ffn(it):
                            b = a_ring.bank(("down", j, 0))
                            dve.wait_ge(a_full[b], a_ring.nth(("down", j, 0), it))
                            t = group_of(it)
                            nc.vector.scalar_tensor_tensor(t, psum[:, b, :], lp[:, PB2:PB2 + 1], t,
                                                           ALU.add, ALU.add).then_inc(a_free[b], 1)
                        if j == 3 and has_front(it):
                            with first_turn_of_layer(dve, it):
                                split_w1(it)

                nc.vector.memset(bd[:, :, :], 0.0)
                nc.vector.memset(kbd[:, :, :, :], 0.0)
                nc.vector.memset(xs_hi[:, :, :].bitcast(F32), 0.0)
                nc.vector.memset(xs_lo[:, :, :].bitcast(F32), 0.0)
                nc.vector.memset(xs2[:, :], 0.0)
                nc.vector.memset(eps[:, :], LN_EPS).then_inc(zeroed, 1)
                dve.wait_ge(zeroed, 1)
                shift_split(0, x[:, 0:TILE], 0)
                turn(0)
                with dve.Fori(1, TURNS) as it:
                    turn(it)
                turn(TURNS)

        layers_ctx.close()
        xin = sbuf(root, "xin", [P, TOK])
        xin_loaded = [sem(f"xin_loaded{g}") for g in range(GROUPS)]
        added, stored = sem("added"), sem("stored")
        with nc.Block() as block:
            @block.vector
            def _(dve):
                for g in range(GROUPS):
                    t = slice(g * GTOK, (g + 1) * GTOK)
                    dve.wait_ge(xin_loaded[g], 16)
                    nc.vector.tensor_tensor(x[:, t], x[:, t], xin[:, t], ALU.add).then_inc(added, 1)

            @block.sync
            def _(sp):
                for g in range(GROUPS):
                    t = slice(g * GTOK, (g + 1) * GTOK)
                    sp.dma_start(xin[:, t], xT_in[:, t]).then_inc(xin_loaded[g], 16)
                for g in range(GROUPS):
                    t = slice(g * GTOK, (g + 1) * GTOK)
                    sp.wait_ge(added, g + 1)
                    sp.dma_start(out[:, t], x[:, t]).then_inc(stored, 16)
                sp.wait_ge(stored, GROUPS * 16)


def _rope_tables(np):
    f = np.float32
    half = np.arange(0, HD, 2, dtype=f)
    inv_freq = (f(1.0) / f(10000.0) ** (half / f(HD))).astype(f)
    t = np.arange(SEQ, dtype=f)
    freqs = t[:, None] * inv_freq[None, :]
    freqs = np.concatenate([freqs, freqs], -1)
    base_scale = (half + f(0.4 * HD)) / f(1.4 * HD)
    power = (t - SEQ // 2) / f(16)
    scale = (base_scale[None, :] ** power[:, None]).astype(f)
    scale = np.concatenate([scale, scale], -1)
    sign = np.concatenate([np.ones(HD // 2, f), -np.ones(HD // 2, f)])
    cos, sin = np.cos(freqs).astype(f), (np.sin(freqs) * sign).astype(f)
    tabs = np.stack([cos * scale * f(8), sin * scale * f(8), cos / scale, sin / scale], 1)
    return np.ascontiguousarray(np.tile(tabs, (TB, 1, 1)).astype(f))


def kernel(x, itok_B_0_2, L0_cond_wi, L0_cond_wo, L0_cond_swi, L0_cond_swo, L0_cond_g1, L0_cond_g2,
           L0_ffn_Wqkv, L0_ffn_q_scale, L0_ffn_k_scale, L0_ffn_Wo, L0_ffn_ln_g, L0_ffn_ln_b,
           L0_ffn_W1, L0_ffn_b1, L0_ffn_W2, L0_ffn_b2):
    import numpy as np
    import concourse.bacc as bacc
    from concourse.bass_utils import run_bass_kernel_spmd

    def a(v):
        return np.asarray(v)

    b1 = a(L0_ffn_b1)
    params = np.zeros((P, LAYERS, NPAR), b1.dtype)
    params[:, :, PG], params[:, :, PB], params[:, :, PB2] = a(L0_ffn_ln_g).T, a(L0_ffn_ln_b).T, a(L0_ffn_b2).T
    for c, (off, w) in enumerate(FC):
        params[:w, :, PBA + c] = b1[:, off:off + w].T
        params[:w, :, PBG + c] = b1[:, DI + off:DI + off + w].T
    w2 = np.zeros((3 * P, LAYERS, DIM), np.float32)
    w2[:DI] = a(L0_ffn_W2).transpose(1, 0, 2)
    i, j = np.arange(P)[:, None] % SEQ, np.arange(SEQ)[None, :]
    arrays = {
        "xT_in": a(x).reshape(TOK, DIM).T,
        "label": a(itok_B_0_2),
        "wi": a(L0_cond_wi).transpose(1, 0, 2),
        "wo": a(L0_cond_wo).reshape(EXPERTS, EC, P, DIM).transpose(2, 0, 1, 3),
        "swi": a(L0_cond_swi).transpose(1, 0, 2),
        "swo": a(L0_cond_swo).reshape(SHARED, EC, P, DIM).transpose(2, 0, 1, 3),
        "g1": a(L0_cond_g1).reshape(3, DIM, DIM).transpose(1, 0, 2),
        "g2": a(L0_cond_g2),
        "wqkv": a(L0_ffn_Wqkv).transpose(1, 0, 2),
        "qk_scale": np.stack([a(L0_ffn_q_scale), a(L0_ffn_k_scale)], 1),
        "wout": a(L0_ffn_Wo).reshape(LAYERS, HP, P, DIM).transpose(2, 0, 1, 3),
        "w1": a(L0_ffn_W1).transpose(1, 0, 2),
        "w2": w2.reshape(3, P, LAYERS, DIM).transpose(1, 2, 0, 3),
        "params": params,
        "rope": _rope_tables(np),
        "mask": np.tile(np.concatenate([np.where(j > i, np.float32(NEG), np.float32(0)),
                                        np.zeros((P, SEQ), np.float32)], 1), (1, 512 // (2 * SEQ))),
        "ident": np.eye(P, dtype=np.float32),
    }
    nc = bacc.Bacc("TRN2", target_bir_lowering=False, num_devices=1)
    sent, args = {}, []
    for name, v in arrays.items():
        v = np.ascontiguousarray(v)
        sent[f"{name}_dram"] = v
        args.append(nc.dram_tensor(f"{name}_dram", v.shape, mybir.dt.from_np(v.dtype), kind="ExternalInput").ap())
    args.append(nc.dram_tensor("out_dram", (DIM, TOK), F32, kind="ExternalOutput").ap())
    build(nc, *args)
    r = run_bass_kernel_spmd(nc, [sent], core_ids=[0])
    return np.ascontiguousarray(r.results[0]["out_dram"].T).reshape(BATCH, SEQ, DIM)
```

```python
from contextlib import ExitStack, nullcontext

import concourse.bass as bass
from concourse import mybir

F32 = mybir.dt.float32
F32R = mybir.dt.float32r
BF16 = mybir.dt.bfloat16
I32 = mybir.dt.int32
ALU = mybir.AluOpType
ACT = mybir.ActivationFunctionType
AX_X = mybir.AxisListType.X

P = 128
BATCH, SEQ, DIM = 128, 32, 128
TOK = BATCH * SEQ
TILE = 128
TB = TILE // SEQ
GTOK = 512
GT = GTOK // TILE
GROUPS = TOK // GTOK
GB = GTOK // SEQ
LAYERS, HEADS, HD = 6, 16, 64
HP = HEADS // 2
INNER = HEADS * HD
DI = 341
FC = [(0, 128), (128, 128), (256, 85)]
EXPERTS, SHARED, EF = 5, 2, 512
EC = EF // P
TURNS = LAYERS * GROUPS
NEG = -1e30
LN_EPS = 1e-5
SS_SCALE = float(2 ** 20)
Y_SCALE = float(2 ** 10)
LN_EXP_SET = "natural_log_exp_and_others"
PG, PB, PB2, PBA, PBG, NPAR = 0, 1, 2, 3, 6, 9


def known(count):
    return max(count, 0) if isinstance(count, int) else count


def has_front(it):
    return not (isinstance(it, int) and it == TURNS)


def has_cd(it, j):
    if isinstance(it, int):
        return j >= 1 if it == 0 else j == 0
    return True


def has_ef(it, j):
    if isinstance(it, int):
        return j >= 2 if it == 0 else j < 2
    return True


def has_ffn(it):
    return not (isinstance(it, int) and it == 0)


def has_use(key, it):
    kind, j = key[0], key[1]
    if kind == "qkv":
        return has_front(it)
    if kind == "qkT":
        return has_cd(it, j)
    if kind in ("av", "wo"):
        return has_ef(it, j)
    return has_ffn(it)


def layer_of(it):
    layer = it >> 3
    return layer if isinstance(layer, int) else layer.with_bounds(min_val=0, max_val=LAYERS - 1)


def at_layer_change(eng, it):
    return nullcontext() if isinstance(it, int) else eng.If(((it + 1) & (GROUPS - 1)) < 2)


def first_turn_of_layer(eng, it):
    return nullcontext() if isinstance(it, int) else eng.If((it & (GROUPS - 1)) < 1)


def last_turn_of_layer(eng, it):
    return eng.If((it & (GROUPS - 1)) > GROUPS - 2)


def not_last_layer(eng, it):
    return eng.If(it < TURNS - GROUPS)


class Ring:

    def __init__(self, banks, keys):
        self.n, self.keys = banks, keys

    def bank(self, key):
        return self.keys.index(key) % self.n

    def nth(self, key, it):
        bank = self.bank(key)
        here = [k for k in self.keys[bank::self.n] if k is not None]
        upto = here[:here.index(key) + 1]
        first = sum(has_use(k, 0) for k in here)
        if isinstance(it, int) and it == 0:
            return sum(has_use(k, 0) for k in upto)
        if isinstance(it, int):
            return first + (TURNS - 1) * len(here) + sum(has_use(k, it) for k in upto)
        return it * len(here) + (first - len(here) + len(upto))


def a_ring_keys():
    keys = []
    for j in range(GT):
        keys += [("qkv", j, c) for c in range(6)]
        if j == 3:
            keys += [None, None] + [("up", j, c) for c in range(6)] + [None, None, ("down", j, 0), None]
    return keys


def x_ring_keys():
    keys = []
    for j in range(GT):
        keys += [("qkT", j, f) for f in range(4)]
        if j == 2:
            keys += [("mean", j, 0)]
        keys += [("av", j, 0), ("av", j, 1)]
        if j == 2:
            keys += [("var", j, 0)]
        keys += [("wo", j, 0)]
    return keys


def build(nc, xT_in, label, wi, wo, swi, swo, g1, g2, wqkv, qk_scale, wout, w1, w2, params,
          rope, mask, ident, out):
    root = ExitStack()
    with root:
        def sem(name):
            return root.enter_context(nc.semaphore(name))

        def sbuf(ctx, name, shape, dt=F32):
            return ctx.enter_context(nc.sbuf_tensor(name, shape, dt))

        psum = root.enter_context(nc.psum_tensor("psum", [P, 8, 512], F32))
        x = sbuf(root, "x", [P, TOK])
        ident_sb = sbuf(root, "ident_sb", [P, P])
        ident_bf = sbuf(root, "ident_bf", [P, P], BF16)
        mask_sb = sbuf(root, "mask_sb", [P, SEQ])
        mask_bf = sbuf(root, "mask_bf", [P, 8, SEQ], BF16)
        mean_w = sbuf(root, "mean_w", [P, P])
        base = sbuf(root, "base", [P, 4, HD])
        scl = sbuf(root, "scl", [P, LAYERS, 2, HD])
        par = sbuf(root, "par", [P, LAYERS, NPAR])
        wqkv_sb = sbuf(root, "wqkv_sb", [P, 3 * INNER])
        wout_sb = sbuf(root, "wout_sb", [P, HP, DIM])
        w1_sb = sbuf(root, "w1_sb", [P, 2 * DI])
        w2_sb = sbuf(root, "w2_sb", [P, 3, DIM])

        wqkv_hi = sbuf(root, "wqkv_hi", [P, 3 * INNER], F32R)
        wqkv_lo = sbuf(root, "wqkv_lo", [P, 3 * INNER], F32R)
        tab = sbuf(root, "tab", [P, 4, HD])

        wqkv_hi_done, wqkv_lo_done = sem("wqkv_hi_done"), sem("wqkv_lo_done")
        tab_done = sem("tab_done")
        const_loaded = sem("const_loaded")
        wqkv_loaded, wout_loaded = sem("wqkv_loaded"), sem("wout_loaded")
        w1_loaded = sem("w1_loaded")
        w2_loaded = sem("w2_loaded")

        def load_wqkv(eng, layer):
            return eng.dma_start(wqkv_sb[:, :].unsqueeze(1), wqkv[:, bass.ds(layer, 1), :]).then_inc(wqkv_loaded, 16)

        def load_wout(eng, layer):
            return eng.dma_start(wout_sb[:, :, :].unsqueeze(1),
                                 wout[:, bass.ds(layer, 1), :, :]).then_inc(wout_loaded, 16)

        def load_w1(eng, layer):
            eng.dma_start(w1_sb[:, :].unsqueeze(1), w1[:, bass.ds(layer, 1), :]).then_inc(w1_loaded, 16)

        def load_w2(eng, layer):
            eng.dma_start(w2_sb[:, 0:2, :].unsqueeze(1), w2[:, bass.ds(layer, 1), 0:2, :]).then_inc(w2_loaded, 16)
            eng.dma_start(w2_sb[0:85, 2:3, :].unsqueeze(1),
                          w2[0:85, bass.ds(layer, 1), 2:3, :]).then_inc(w2_loaded, 16)

        def wqkv_high(eng, layer, c):
            eng.wait_ge(wqkv_loaded, (layer + 1) * 16)
            w = slice(c * 512, (c + 1) * 512)
            nc.scalar.copy(wqkv_hi[:, w], wqkv_sb[:, w]).then_inc(wqkv_hi_done, 1)

        def wqkv_low(eng, layer, c):
            eng.wait_ge(wqkv_hi_done, layer * 6 + c + 1)
            w = slice(c * 512, (c + 1) * 512)
            nc.vector.tensor_tensor(wqkv_lo[:, w], wqkv_sb[:, w], wqkv_hi[:, w].bitcast(F32),
                                    ALU.subtract).then_inc(wqkv_lo_done, 1)

        def tables(eng, layer):
            for qk in range(2):
                s = scl[:, bass.ds(layer, 1), qk, :]
                last = nc.vector.tensor_tensor(tab[:, 2 * qk:2 * qk + 2, :], base[:, 2 * qk:2 * qk + 2, :],
                                               s.to_broadcast([P, 2, HD]), ALU.mult)
            last.then_inc(tab_done, 1)
            eng.wait_ge(tab_done, layer + 1)

        NE = SHARED + EXPERTS
        NK = NE * EC
        PER = NK // 4
        RAW = 3
        cond_ctx = ExitStack()
        with cond_ctx as ctx:
            w_raw = sbuf(ctx, "w_raw", [P, RAW, 2, EF])
            wi_hi, wi_lo = sbuf(ctx, "wi_hi", [P, NE, EF], F32R), sbuf(ctx, "wi_lo", [P, NE, EF], F32R)
            wo_hi = sbuf(ctx, "wo_hi", [P, NE, EC * DIM], F32R)
            wo_lo = sbuf(ctx, "wo_lo", [P, NE, EC * DIM], F32R)
            g1_sb = sbuf(ctx, "g1_sb", [P, 3, DIM])
            g2_sb = sbuf(ctx, "g2_sb", [P, 3])
            g2_wide = sbuf(ctx, "g2_wide", [P, 3, P])
            lab_i = sbuf(ctx, "lab_i", [P, BATCH], I32)
            lab = sbuf(ctx, "lab", [P, BATCH])
            lab_low = sbuf(ctx, "lab_low", [P, BATCH])
            lab_wrapped = sbuf(ctx, "lab_wrapped", [P, BATCH])
            picked = sbuf(ctx, "picked", [P, EXPERTS, BATCH])
            x_hi, x_lo = sbuf(ctx, "x_hi", [P, GTOK], F32R), sbuf(ctx, "x_lo", [P, GTOK], F32R)
            xm_hi = sbuf(ctx, "xm_hi", [P, 2, GTOK], F32R)
            xm_lo = sbuf(ctx, "xm_lo", [P, 2, GTOK], F32R)
            hid_hi = sbuf(ctx, "hid_hi", [P, 4, GTOK], F32R)
            hid_lo = sbuf(ctx, "hid_lo", [P, 4, GTOK], F32R)
            outs = sbuf(ctx, "outs", [P, 3, GTOK])
            ghid = sbuf(ctx, "ghid", [P, GB])
            logit = sbuf(ctx, "logit", [P, 3, GB])
            gmax = sbuf(ctx, "gmax", [P, GB])
            gdiff = sbuf(ctx, "gdiff", [P, 3, GB])
            gexp = sbuf(ctx, "gexp", [P, 3, GB])
            gsum = sbuf(ctx, "gsum", [P, GB])
            grec = sbuf(ctx, "grec", [P, GB])
            gw = sbuf(ctx, "gw", [P, 3, GB])
            part = sbuf(ctx, "part", [P, 3, GTOK])
            part01 = sbuf(ctx, "part01", [P, GTOK])

            x_loaded, x_rest_loaded = sem("x_loaded"), sem("x_rest_loaded")
            w_loaded = [sem(f"w_loaded{q}") for q in range(NE)]
            small_loaded = sem("small_loaded")
            setup = sem("setup")
            picked_done = sem("picked_done")
            w_hi_done, w_lo_done = sem("w_hi_done"), sem("w_lo_done")
            x_hi_done, x_split = sem("x_hi_done"), sem("x_split")
            xm_ready = sem("xm_ready")
            up_full = [sem(f"up_full{b}") for b in range(4)]
            hid_hi_done = [sem(f"hid_hi_done{b}") for b in range(4)]
            hid_full = [sem(f"hid_full{b}") for b in range(4)]
            hid_used = [sem(f"hid_used{b}") for b in range(4)]
            routed_out, shared_out = sem("routed_out"), sem("shared_out")
            ghid_done, ghid_ready = sem("ghid_done"), sem("ghid_ready")
            logit_done, gdiff_ready, gexp_ready = sem("logit_done"), sem("gdiff_ready"), sem("gexp_ready")
            gate_step, part_step = sem("gate_step"), sem("part_step")
            combined = sem("combined")
            GATE_STEPS = 5
            HID_AT, LOGIT_AT = 4, 8
            OUT_AT, GATE_AT, SPLIT_AT = 20, 12, 24
            WQKV_AT = 18

            def out_of(q):
                return q + 1 if q < SHARED else 0

            with nc.Block() as block:
                @block.sync
                def _(sp):
                    sp.dma_start(x[:, 0:GTOK], xT_in[:, 0:GTOK]).then_inc(x_loaded, 16)
                    for q in range(NE):
                        up, down = (swi[:, q, :], swo[:, q, :, :]) if q < SHARED else (
                            wi[:, q - SHARED, :], wo[:, q - SHARED, :, :])
                        if q == RAW:
                            load_wqkv(sp, 0)
                        if q >= RAW:
                            sp.wait_ge(w_lo_done, q - RAW + 1)
                        sp.dma_start(w_raw[:, q % RAW, 0, :], up).then_inc(w_loaded[q], 16)
                        sp.dma_start(w_raw[:, q % RAW, 1, :],
                                     down.rearrange("p c d -> p (c d)")).then_inc(w_loaded[q], 16)
                    sp.dma_start(x[:, GTOK:], xT_in[:, GTOK:]).then_inc(x_rest_loaded, 16)
                    sp.dma_start(ident_sb[:, :], ident).then_inc(const_loaded, 16)
                    sp.dma_start(mask_sb[:, :], mask).then_inc(const_loaded, 16)
                    sp.dma_start(base[:, :, :], rope).then_inc(const_loaded, 16)
                    sp.dma_start(scl[:, :, :, :], qk_scale.unsqueeze(0).to_broadcast(
                        [P, LAYERS, 2, HD])).then_inc(const_loaded, 16)
                    sp.dma_start(par[:, :, :], params).then_inc(const_loaded, 16)
                    load_wout(sp, 0)
                    load_w1(sp, 0)
                    load_w2(sp, 0)

                @block.gpsimd
                def _(pool):
                    def mask_tokens(g):
                        pool.wait_ge(x_split, g + 1)
                        for e in range(EXPERTS):
                            if e >= 2:
                                pool.wait_ge(up_full[3], g * PER + SHARED + e - 1)
                            else:
                                pool.wait_ge(up_full[3], g * PER)
                            m = picked[:, e, bass.ds(g * GB, GB)].unsqueeze(2).to_broadcast([P, GB, SEQ])
                            for dst, src in ((xm_hi, x_hi), (xm_lo, x_lo)):
                                last = nc.gpsimd.tensor_tensor(
                                    dst[:, e % 2, :].rearrange("p (b s) -> p b s", s=SEQ),
                                    src[:, :].bitcast(F32).rearrange("p (b s) -> p b s", s=SEQ), m, ALU.mult)
                            last.then_inc(xm_ready, 1)

                    pool.wait_ge(picked_done, 1)
                    mask_tokens(0)
                    with pool.Fori(1, GROUPS) as g:
                        mask_tokens(g)

                @block.tensor
                def _(pe):
                    def three(out_ap, w_hi, w_lo, m_hi, m_lo, start, stop):
                        nc.tensor.matmul(out_ap, w_hi, m_hi, start=start, stop=False)
                        nc.tensor.matmul(out_ap, w_hi, m_lo, start=False, stop=False)
                        return nc.tensor.matmul(out_ap, w_lo, m_hi, start=False, stop=stop)

                    def gate_hidden(g):
                        pe.wait_ge(shared_out, (g + 1) * 2)
                        pe.wait_ge(routed_out, g + 1)
                        for c in range(3):
                            first = outs[:, c, :].rearrange("p (b s) -> p b s", s=SEQ)[:, :, 0]
                            last = nc.tensor.matmul(psum[:, 7, 0:GB], g1_sb[:, c, :], first,
                                                    start=c == 0, stop=c == 2)
                        last.then_inc(ghid_done, 1)

                    def gate_logits(g):
                        pe.wait_ge(ghid_ready, g + 1)
                        for c in range(3):
                            last = nc.tensor.matmul(psum[:, 7, GB * (c + 1):GB * (c + 2)], g2_wide[:, c, :],
                                                    ghid[:, :], start=True, stop=True)
                        last.then_inc(logit_done, 1)

                    def experts(g, later):
                        for k in range(NK + 2):
                            if k < NK:
                                q, f, b = k // EC, k % EC, k % 4
                                if k == 0:
                                    pe.wait_ge(x_split, g + 1)
                                if not later and f == 0:
                                    pe.wait_ge(w_lo_done, q + 1)
                                if q >= SHARED and f == 0:
                                    pe.wait_ge(xm_ready, g * EXPERTS + q - SHARED + 1)
                                if later or k >= 4:
                                    pe.wait_ge(hid_full[b], g * PER + k // 4)
                                m_hi, m_lo = (x_hi[:, :], x_lo[:, :]) if q < SHARED else (
                                    xm_hi[:, (q - SHARED) % 2, :], xm_lo[:, (q - SHARED) % 2, :])
                                w = slice(f * P, (f + 1) * P)
                                three(psum[:, b, :], wi_hi[:, q, w], wi_lo[:, q, w], m_hi, m_lo,
                                      True, True).then_inc(up_full[b], 1)
                            if k >= 2:
                                q, f, b = (k - 2) // EC, (k - 2) % EC, (k - 2) % 4
                                if later and k == 2:
                                    pe.wait_ge(shared_out, g * 2)
                                if later and k - 2 == SHARED * EC:
                                    pe.wait_ge(routed_out, g)
                                pe.wait_ge(hid_full[b], g * PER + (k - 2) // 4 + 1)
                                w = slice(f * DIM, (f + 1) * DIM)
                                three(psum[:, 4 + out_of(q), :], wo_hi[:, q, w], wo_lo[:, q, w],
                                      hid_hi[:, b, :], hid_lo[:, b, :], f == 0 and q <= SHARED,
                                      f == EC - 1 and (q < SHARED or q == NE - 1)).then_inc(hid_used[b], 1)
                            if later and k == HID_AT:
                                gate_hidden(g - 1)
                            if later and k == LOGIT_AT:
                                gate_logits(g - 1)

                    pe.wait_ge(small_loaded, 48)
                    pe.wait_ge(setup, 2)
                    experts(0, False)
                    with pe.Fori(1, GROUPS) as g:
                        experts(g, True)
                    gate_hidden(GROUPS - 1)
                    gate_logits(GROUPS - 1)

                @block.scalar
                def _(act):
                    def split_expert(q):
                        act.wait_ge(w_loaded[q], 32)
                        nc.scalar.copy(wi_hi[:, q, :], w_raw[:, q % RAW, 0, :])
                        nc.scalar.copy(wo_hi[:, q, :], w_raw[:, q % RAW, 1, :]).then_inc(w_hi_done, 1)

                    def gate_relu(g):
                        act.wait_ge(ghid_done, g + 1)
                        nc.scalar.activation(ghid[:, :], psum[:, 7, 0:GB], ACT.Relu).then_inc(ghid_ready, 1)

                    def gate_exp(g):
                        act.wait_ge(gdiff_ready, g + 1)
                        nc.scalar.activation(gexp[:, :, :], gdiff[:, :, :], ACT.Exp).then_inc(gexp_ready, 1)

                    def experts(g, later):
                        for k in range(NK):
                            b = k % 4
                            if not later and b == 0 and k // EC + 1 < NE:
                                split_expert(k // EC + 1)
                            if not later and k >= WQKV_AT and k < WQKV_AT + 6:
                                wqkv_high(act, 0, k - WQKV_AT)
                            act.wait_ge(up_full[b], g * PER + k // 4 + 1)
                            if later or k >= 4:
                                act.wait_ge(hid_used[b], g * PER + k // 4)
                            nc.scalar.activation(hid_hi[:, b, :], psum[:, b, :], ACT.Relu).then_inc(hid_hi_done[b], 1)
                            if later and k == HID_AT + 1:
                                gate_relu(g - 1)
                            if later and k == GATE_AT:
                                gate_exp(g - 1)
                            if k == OUT_AT:
                                if later:
                                    act.wait_ge(combined, g)
                                act.wait_ge(hid_used[3], g * PER + SHARED)
                                for o in (1, 2):
                                    nc.scalar.copy(outs[:, o, :], psum[:, 4 + o, :]).then_inc(shared_out, 1)

                    act.dma_start(lab_i[:, :], label.unsqueeze(0).to_broadcast([P, BATCH])).then_inc(small_loaded, 16)
                    act.dma_start(g1_sb[:, :, :], g1).then_inc(small_loaded, 16)
                    act.dma_start(g2_sb[:, :], g2).then_inc(small_loaded, 16)
                    split_expert(0)
                    experts(0, False)
                    with act.Fori(1, GROUPS) as g:
                        experts(g, True)
                    gate_relu(GROUPS - 1)
                    gate_exp(GROUPS - 1)

                @block.vector
                def _(dve):
                    n = [0]

                    def prepared(ins):
                        n[0] += 1
                        ins.then_inc(setup, 1)
                        dve.wait_ge(setup, n[0])

                    def split_x(g):
                        if not isinstance(g, int) or g > 0:
                            dve.wait_ge(xm_ready, g * EXPERTS)
                            dve.wait_ge(up_full[3], g * PER - EXPERTS)
                        t = x[:, bass.ds((g & (GROUPS - 1)) * GTOK, GTOK)]
                        nc.vector.tensor_copy(x_hi[:, :], t).then_inc(x_hi_done, 1)
                        dve.wait_ge(x_hi_done, g + 1)
                        nc.vector.tensor_tensor(x_lo[:, :], t, x_hi[:, :].bitcast(F32),
                                                ALU.subtract).then_inc(x_split, 1)

                    def split_expert(q):
                        dve.wait_ge(w_hi_done, q + 1)
                        for i, (lo, hi) in enumerate(((wi_lo, wi_hi), (wo_lo, wo_hi))):
                            last = nc.vector.tensor_tensor(lo[:, q, :], w_raw[:, q % RAW, i, :],
                                                           hi[:, q, :].bitcast(F32), ALU.subtract)
                        last.then_inc(w_lo_done, 1)

                    def gate(g):
                        steps = [0]

                        def stepped(ins):
                            steps[0] += 1
                            ins.then_inc(gate_step, 1)
                            dve.wait_ge(gate_step, g * GATE_STEPS + steps[0])

                        dve.wait_ge(logit_done, g + 1)
                        stepped(nc.vector.tensor_copy(logit[:, :, :], psum[:, 7, GB:4 * GB].rearrange(
                            "p (o b) -> p o b", b=GB)))
                        stepped(nc.vector.tensor_reduce(gmax[:, :], logit[:, :, :].rearrange("p o b -> p b o"),
                                                        AX_X, ALU.max))
                        nc.vector.tensor_tensor(gdiff[:, :, :], logit[:, :, :],
                                                gmax[:, :].unsqueeze(1).to_broadcast([P, 3, GB]),
                                                ALU.subtract).then_inc(gdiff_ready, 1)
                        dve.wait_ge(gexp_ready, g + 1)
                        stepped(nc.vector.tensor_reduce(gsum[:, :], gexp[:, :, :].rearrange("p o b -> p b o"),
                                                        AX_X, ALU.add))
                        stepped(nc.vector.reciprocal(grec[:, :], gsum[:, :]))
                        stepped(nc.vector.tensor_tensor(gw[:, :, :], gexp[:, :, :],
                                                        grec[:, :].unsqueeze(1).to_broadcast([P, 3, GB]), ALU.mult))
                        assert steps[0] == GATE_STEPS

                    def weigh(g, step):
                        wide = "p (b s) -> p b s"
                        if step < 3:
                            dve.wait_ge(shared_out, (g + 1) * 2)
                            nc.vector.tensor_tensor(
                                part[:, step, :].rearrange(wide, s=SEQ), outs[:, step, :].rearrange(wide, s=SEQ),
                                gw[:, step, :].unsqueeze(2).to_broadcast([P, GB, SEQ]), ALU.mult).then_inc(part_step, 1)
                        elif step == 3:
                            dve.wait_ge(part_step, g * 4 + 2)
                            nc.vector.tensor_tensor(part01[:, :], part[:, 0, :], part[:, 1, :],
                                                    ALU.add).then_inc(part_step, 1)
                        else:
                            dve.wait_ge(part_step, g * 4 + 4)
                            nc.vector.tensor_tensor(x[:, bass.ds(g * GTOK, GTOK)], part01[:, :],
                                                    part[:, 2, :], ALU.add).then_inc(combined, 1)

                    def experts(g, later):
                        for k in range(NK):
                            b = k % 4
                            dve.wait_ge(hid_hi_done[b], g * PER + k // 4 + 1)
                            nc.vector.scalar_tensor_tensor(hid_lo[:, b, :], psum[:, b, :], 0.0,
                                                           hid_hi[:, b, :].bitcast(F32), ALU.max,
                                                           ALU.subtract).then_inc(hid_full[b], 1)
                            if not later and b == 0 and k // EC + 1 < NE:
                                split_expert(k // EC + 1)
                            if not later and k >= WQKV_AT and k < WQKV_AT + 6:
                                wqkv_low(dve, 0, k - WQKV_AT)
                            if not later and k == WQKV_AT + 7:
                                dve.wait_ge(const_loaded, 80)
                                tables(dve, 0)
                                prepared(nc.vector.tensor_copy(ident_bf[:, :], ident_sb[:, :]))
                                prepared(nc.vector.tensor_copy(
                                    mask_bf[:, :, :], mask_sb[:, :].unsqueeze(1).to_broadcast([P, 8, SEQ])))
                            if later and k == GATE_AT:
                                gate(g - 1)
                            if later and k > GATE_AT and k <= GATE_AT + 5:
                                weigh(g - 1, k - GATE_AT - 1)
                            if not later and k == SPLIT_AT:
                                dve.wait_ge(x_rest_loaded, 16)
                            if k == SPLIT_AT:
                                split_x(g + 1)
                        for b in range(4):
                            dve.wait_ge(hid_used[b], (g + 1) * PER)
                        nc.vector.tensor_copy(outs[:, 0, :], psum[:, 4, :]).then_inc(routed_out, 1)

                    prepared(nc.vector.memset(mean_w[:, :], 1.0 / DIM))
                    dve.wait_ge(small_loaded, 48)
                    prepared(nc.vector.tensor_copy(g2_wide[:, :, :], g2_sb[:, :].unsqueeze(2).to_broadcast([P, 3, P])))
                    prepared(nc.vector.tensor_copy(lab[:, :], lab_i[:, :]))
                    prepared(nc.vector.tensor_scalar(lab_low[:, :], lab[:, :], 0.0, float(EXPERTS),
                                                     ALU.is_lt, ALU.mult))
                    prepared(nc.vector.tensor_tensor(lab_wrapped[:, :], lab[:, :], lab_low[:, :], ALU.add))
                    prepared(nc.vector.tensor_scalar(lab[:, :], lab_wrapped[:, :], 0.0, float(EXPERTS - 1),
                                                     ALU.max, ALU.min))
                    for e in range(EXPERTS):
                        last = nc.vector.tensor_scalar(picked[:, e, :], lab[:, :], float(e), None, ALU.is_equal)
                    last.then_inc(picked_done, 1)
                    dve.wait_ge(x_loaded, 16)
                    split_x(0)
                    split_expert(0)
                    experts(0, False)
                    with dve.Fori(1, GROUPS) as g:
                        experts(g, True)
                    gate(GROUPS - 1)
                    for step in range(5):
                        weigh(GROUPS - 1, step)

        layers_ctx = ExitStack()
        ctx = layers_ctx
        xs_hi = sbuf(ctx, "xs_hi", [P, 2, TILE], F32R)
        xs_lo = sbuf(ctx, "xs_lo", [P, 2, TILE], F32R)
        w1_hi = sbuf(ctx, "w1_hi", [P, 2 * DI], F32R)
        w1_lo = sbuf(ctx, "w1_lo", [P, 2 * DI], F32R)
        lp = sbuf(ctx, "lp", [P, NPAR])
        sq = sbuf(ctx, "sq", [P, 4, 512])
        rcos = sbuf(ctx, "rcos", [P, 2, 4, 512])
        rsin = sbuf(ctx, "rsin", [P, 4, 512])
        ss = sbuf(ctx, "ss", [P, 2, 2 * HEADS])
        ssc = sbuf(ctx, "ssc", [P, 2, 2 * HEADS])
        lns = sbuf(ctx, "lns", [P, 2 * HEADS])
        y0 = sbuf(ctx, "y0", [P, 2, 2 * HEADS])
        nt_a = sbuf(ctx, "nt_a", [P, 2 * HEADS])
        nt_b = sbuf(ctx, "nt_b", [P, 2 * HEADS])
        rn = sbuf(ctx, "rn", [P, 2, 2 * HEADS])
        v_sb = sbuf(ctx, "v_sb", [P, 4, INNER])
        qT = sbuf(ctx, "qT", [P, HP, TILE])
        kbd = sbuf(ctx, "kbd", [P, HP, 2, TILE + SEQ])
        mx = sbuf(ctx, "mx", [P, HEADS])
        s_sb = sbuf(ctx, "s_sb", [P, HEADS, SEQ])
        p_sb = sbuf(ctx, "p_sb", [P, HEADS, SEQ])
        sums = sbuf(ctx, "sums", [P, HEADS])
        rinv = sbuf(ctx, "rinv", [P, HEADS])
        pT = sbuf(ctx, "pT", [P, HEADS, SEQ])
        bd = sbuf(ctx, "bd", [P, HEADS, TILE])
        oT = sbuf(ctx, "oT", [P, HP, TILE])
        xs2 = sbuf(ctx, "xs2", [P, GTOK])
        xc = sbuf(ctx, "xc", [P, GTOK])
        xsq = sbuf(ctx, "xsq", [P, GTOK])
        lnv = sbuf(ctx, "lnv", [P, GTOK])
        rstd = sbuf(ctx, "rstd", [P, GTOK])
        xg = sbuf(ctx, "xg", [P, GTOK])
        xn_hi = sbuf(ctx, "xn_hi", [P, GTOK], F32R)
        xn_lo = sbuf(ctx, "xn_lo", [P, GTOK], F32R)
        gel = sbuf(ctx, "gel", [P, 3, GTOK])
        h = sbuf(ctx, "h", [P, 3, GTOK])
        eps = sbuf(ctx, "eps", [P, 1])

        a_ring, x_ring = Ring(4, a_ring_keys()), Ring(2, x_ring_keys())
        a_full, a_free = [sem(f"a_full{b}") for b in range(4)], [sem(f"a_free{b}") for b in range(4)]
        x_full, x_free = [sem(f"x_full{b}") for b in range(2)], [sem(f"x_free{b}") for b in range(2)]
        X0, S0 = 4, 6

        zeroed, pads_zeroed = sem("zeroed"), sem("pads_zeroed")
        w1_hi_done, w1_lo_done = sem("w1_hi_done"), sem("w1_lo_done")
        xs_hi_done = sem("xs_hi_done")
        xs_ready = sem("xs_ready")
        sq_done = sem("sq_done")
        sums_done = sem("sums_done")
        y0_done = sem("y0_done")
        rn_done = sem("rn_done")
        qadd_done, kadd_done = sem("qadd_done"), sem("kadd_done")
        q_ready, k_ready = sem("q_ready"), sem("k_ready")
        scores_done = sem("scores_done")
        s_done = sem("s_done")
        exp_done = sem("exp_done")
        rinv_done = sem("rinv_done")
        pn_done = sem("pn_done")
        pT_done = sem("pT_done")
        bd_done = sem("bd_done")
        dve_norm = sem("dve_norm")
        dve_soft = sem("dve_soft")
        act_norm = sem("act_norm")
        xs2_done = sem("xs2_done")
        xsq_done = sem("xsq_done")
        rstd_done = sem("rstd_done")
        xg_done, xn_hi_done, xn_done = sem("xg_done"), sem("xn_hi_done"), sem("xn_done")

        with nc.Block() as block:
            @block.sync
            def _(sp):
                with sp.Fori(1, LAYERS) as layer:
                    last = layer * GROUPS - 1
                    sp.wait_ge(wqkv_lo_done, layer * 6)
                    load_wqkv(sp, layer)
                    sp.wait_ge(w1_lo_done, layer)
                    load_w1(sp, layer)
                    sp.wait_ge(x_full[x_ring.bank(("wo", 1, 0))], x_ring.nth(("wo", 1, 0), last + 1))
                    load_wout(sp, layer)
                    sp.wait_ge(a_full[a_ring.bank(("down", 3, 0))], a_ring.nth(("down", 3, 0), last + 1))
                    load_w2(sp, layer)

            @block.tensor
            def _(pe):
                def project(it, j, c):
                    n = it * GT + j
                    if c == 0:
                        pe.wait_ge(xs_ready, n + 1)
                    if j == 0:
                        pe.wait_ge(wqkv_lo_done, (it >> 3) * 6 + c + 1)
                    b = a_ring.bank(("qkv", j, c))
                    w = slice(c * 512, (c + 1) * 512)
                    pe.wait_ge(a_free[b], a_ring.nth(("qkv", j, c), it) - 1)
                    nc.tensor.matmul(psum[:, b, :], xs_hi[:, j % 2, :], wqkv_hi[:, w], start=True, stop=False)
                    nc.tensor.matmul(psum[:, b, :], xs_hi[:, j % 2, :], wqkv_lo[:, w], start=False, stop=False)
                    nc.tensor.matmul(psum[:, b, :], xs_lo[:, j % 2, :], wqkv_hi[:, w],
                                     start=False, stop=True).then_inc(a_full[b], 1)

                def transpose_qk(it, j, f):
                    m = it * GT + j - 1
                    if f == 0:
                        pe.wait_ge(q_ready, m + 1)
                    if f == 2:
                        pe.wait_ge(k_ready, m + 1)
                    b = x_ring.bank(("qkT", j, f))
                    pe.wait_ge(x_free[b], x_ring.nth(("qkT", j, f), it) - 1)
                    for i in range(4):
                        last = nc.tensor.transpose(psum[:, X0 + b, i * P:(i + 1) * P],
                                                   rcos[:, (j - 1) % 2, f, i * P:(i + 1) * P], ident_sb[:, :])
                    last.then_inc(x_full[b], 1)

                def score(it, j):
                    m = it * GT + j - 1
                    pe.wait_ge(s_done, known(m))
                    pe.wait_ge(x_free[x_ring.bank(("qkT", j, 2))], x_ring.nth(("qkT", j, 2), it))
                    pe.wait_ge(x_free[x_ring.bank(("qkT", j, 3))], x_ring.nth(("qkT", j, 3), it))
                    for o in range(2):
                        own = psum[:, S0 + o, :].rearrange("p (h w) -> p h w", w=2 * SEQ)[:, :, 0:SEQ]
                        nc.tensor.matmul(own, ident_bf[:, :], mask_bf[:, :, :],
                                         start=True, stop=False, skip_group_check=True)
                    for hp in range(HP):
                        for b in range(TB):
                            col = (hp % 4) * P
                            last = nc.tensor.matmul(
                                psum[SEQ * b:SEQ * (b + 1), S0 + hp // 4, col:col + P],
                                qT[:, hp, SEQ * b:SEQ * (b + 1)], kbd[:, hp, :, SEQ * b:SEQ * (b + 2)],
                                start=False, stop=True, skip_group_check=True)
                    last.then_inc(scores_done, 1)

                def attend(it, j):
                    m = it * GT + j - 2
                    pe.wait_ge(bd_done, known(m + 1))
                    for f in range(2):
                        b = x_ring.bank(("av", j, f))
                        pe.wait_ge(x_free[b], x_ring.nth(("av", j, f), it) - 1)
                        pe.wait_ge(const_loaded, 80)
                        for i in range(4):
                            for odd in range(2):
                                hh = 2 * (4 * f + i) + odd
                                last = nc.tensor.matmul(
                                    psum[64 * odd:64 * odd + 64, X0 + b, i * P:(i + 1) * P],
                                    v_sb[:, (j - 2) % 4, hh * HD:(hh + 1) * HD], bd[:, hh, :],
                                    start=True, stop=True)
                        last.then_inc(x_full[b], 1)

                def project_out(it, j):
                    if j in (0, 2):
                        pe.wait_ge(wout_loaded, known((((it * GT + j - 2) >> 5) + 1) * 16))
                    b = x_ring.bank(("wo", j, 0))
                    pe.wait_ge(x_free[b], x_ring.nth(("wo", j, 0), it) - 1)
                    for hp in range(HP):
                        if hp % 4 == 0:
                            key = ("av", j, hp // 4)
                            pe.wait_ge(x_free[x_ring.bank(key)], x_ring.nth(key, it))
                        last = nc.tensor.matmul(psum[:, X0 + b, 0:TILE], wout_sb[:, hp, :], oT[:, hp, :],
                                                start=hp == 0, stop=hp == HP - 1)
                    last.then_inc(x_full[b], 1)

                def mean(it, key, src, ready):
                    pe.wait_ge(ready, known(it))
                    b = x_ring.bank(key)
                    pe.wait_ge(x_free[b], x_ring.nth(key, it) - 1)
                    nc.tensor.matmul(psum[:, X0 + b, :], mean_w[:, :], src[:, :], start=True,
                                     stop=True).then_inc(x_full[b], 1)

                def ffn_up(it, j):
                    pe.wait_ge(xn_hi_done, it)
                    pe.wait_ge(w1_lo_done, ((it - 1) >> 3) + 1)
                    for c in range(6):
                        off, w = FC[c % 3]
                        off += DI if c < 3 else 0
                        b = a_ring.bank(("up", j, c))
                        pe.wait_ge(a_free[b], a_ring.nth(("up", j, c), it) - 1)
                        nc.tensor.matmul(psum[0:w, b, :], w1_hi[:, off:off + w], xn_hi[:, :], start=True, stop=False)
                        nc.tensor.matmul(psum[0:w, b, :], w1_lo[:, off:off + w], xn_hi[:, :], start=False, stop=False)
                        if c == 0:
                            pe.wait_ge(xn_done, it)
                        nc.tensor.matmul(psum[0:w, b, :], w1_hi[:, off:off + w], xn_lo[:, :], start=False,
                                         stop=True).then_inc(a_full[b], 1)

                def ffn_down(it, j):
                    pe.wait_ge(w2_loaded, (((it - 1) >> 3) + 1) * 32)
                    b = a_ring.bank(("down", j, 0))
                    pe.wait_ge(a_free[b], a_ring.nth(("down", j, 0), it) - 1)
                    for c in (3, 4, 5):
                        pe.wait_ge(a_free[a_ring.bank(("up", j, c))], a_ring.nth(("up", j, c), it))
                    for c in range(3):
                        w = FC[c][1]
                        last = nc.tensor.matmul(psum[:, b, :], w2_sb[0:w, c, :], h[0:w, c, :],
                                                start=c == 0, stop=c == 2)
                    last.then_inc(a_full[b], 1)

                def turn(it):
                    for j in range(GT):
                        for c in range(6):
                            if has_front(it):
                                project(it, j, c)
                            if c < 4 and has_cd(it, j):
                                transpose_qk(it, j, c)
                        if j == 2 and has_ffn(it):
                            mean(it, ("mean", j, 0), xs2, xs2_done)
                        if j == 3 and has_ffn(it):
                            ffn_up(it, j)
                        if has_cd(it, j):
                            score(it, j)
                        if has_ef(it, j):
                            attend(it, j)
                        if j == 3 and has_ffn(it):
                            ffn_down(it, j)
                        if j == 2 and has_ffn(it):
                            mean(it, ("var", j, 0), xsq, xsq_done)
                        if has_ef(it, j):
                            project_out(it, j)

                pe.wait_ge(zeroed, 1)
                turn(0)
                with pe.Fori(1, TURNS) as it:
                    turn(it)
                turn(TURNS)

            @block.scalar
            def _(act):
                def split_w1(it):
                    layer = it >> 3
                    act.wait_ge(w1_loaded, (layer + 1) * 16)
                    if not isinstance(it, int):
                        key = ("up", 3, 5)
                        act.wait_ge(a_full[a_ring.bank(key)], a_ring.nth(key, it))
                    nc.scalar.copy(w1_hi[:, :], w1_sb[:, :]).then_inc(w1_hi_done, 1)

                def square(it, j, c):
                    n = it * GT + j
                    if c == 0:
                        act.wait_ge(sums_done, known(n))
                    b = a_ring.bank(("qkv", j, c))
                    act.wait_ge(a_full[b], a_ring.nth(("qkv", j, c), it))
                    nc.scalar.activation(sq[:, c, :], psum[:, b, :], ACT.Square).then_inc(sq_done, 1)

                def block_diagonal(it, j):
                    m = it * GT + j - 2
                    act.wait_ge(pT_done, known(m + 1))
                    for b in range(TB):
                        t = slice(SEQ * b, SEQ * b + SEQ)
                        last = nc.scalar.copy(bd[t, :, t], pT[t, :, :])
                    last.then_inc(bd_done, 1)

                def values(it, j):
                    for c in (4, 5):
                        b = a_ring.bank(("qkv", j, c))
                        act.wait_ge(a_full[b], a_ring.nth(("qkv", j, c), it))
                        nc.scalar.copy(v_sb[:, j, (c - 4) * 512:(c - 3) * 512],
                                       psum[:, b, :]).then_inc(a_free[b], 1)

                def take_qkT(it, j, f):
                    m = it * GT + j - 1
                    if isinstance(it, int) and m == 0 and f == 0:
                        act.wait_ge(pads_zeroed, 1)
                    if f == 0:
                        act.wait_ge(scores_done, known(m))
                    b = x_ring.bank(("qkT", j, f))
                    pairs = slice(4 * (f % 2), 4 * (f % 2) + 4)
                    act.wait_ge(x_full[b], x_ring.nth(("qkT", j, f), it))
                    src = psum[:, X0 + b, :].rearrange("p (i t) -> p i t", t=TILE)
                    if f < 2:
                        nc.scalar.copy(qT[:, pairs, :], src).then_inc(x_free[b], 1)
                    else:
                        nc.scalar.copy(kbd[0:64, pairs, 0, 0:TILE], src[0:64, :, :])
                        nc.scalar.copy(kbd[64:128, pairs, 1, 0:TILE], src[64:128, :, :]).then_inc(x_free[b], 1)

                def guess_norms(it, j):
                    n = it * GT + j
                    act.wait_ge(sums_done, known(n + 1))
                    nc.scalar.activation(lns[:, :], ssc[:, j % 2, :], ACT.Ln, scale=SS_SCALE).then_inc(act_norm, 1)
                    act.wait_ge(act_norm, known(n + 1))
                    nc.scalar.activation(y0[:, j % 2, :], lns[:, :], ACT.Exp, scale=-0.5).then_inc(y0_done, 1)

                def take_oT(it, j, halves):
                    for f in halves:
                        b = x_ring.bank(("av", j, f))
                        act.wait_ge(x_full[b], x_ring.nth(("av", j, f), it))
                        nc.scalar.copy(oT[:, 4 * f:4 * f + 4, :], psum[:, X0 + b, :].rearrange(
                            "p (i t) -> p i t", t=TILE)).then_inc(x_free[b], 1)

                def exponentials(it, j):
                    m = it * GT + j - 1
                    act.wait_ge(s_done, known(m + 1))
                    nc.scalar.activation(p_sb[:, :, :], s_sb[:, :, :], ACT.Exp).then_inc(exp_done, 1)

                def turn(it):
                    for j in range(GT):
                        for c in range(4):
                            if c < 3 and has_front(it):
                                square(it, j, c)
                            if has_cd(it, j):
                                take_qkT(it, j, c)
                        if has_front(it):
                            square(it, j, 3)
                        if j < 3 and has_ef(it, j):
                            block_diagonal(it, j)
                        if has_front(it):
                            values(it, j)
                        if j == 3 and has_ffn(it):
                            for c in range(3):
                                w = FC[c][1]
                                b = a_ring.bank(("up", j, c))
                                act.wait_ge(a_full[b], a_ring.nth(("up", j, c), it))
                                nc.scalar.activation(gel[0:w, c, :], psum[0:w, b, :], ACT.Gelu,
                                                     bias=lp[0:w, PBG + c:PBG + c + 1]
                                                     ).then_inc(a_free[b], 1)
                            nc.scalar.preload_act_table_set(LN_EXP_SET)
                        if j == 3 and has_ef(it, j):
                            block_diagonal(it, j)
                        if j == 2 and has_ffn(it):
                            b = x_ring.bank(("mean", j, 0))
                            act.wait_ge(x_free[b], x_ring.nth(("mean", j, 0), it))
                            nc.scalar.activation(xsq[:, :], xc[:, :], ACT.Square).then_inc(xsq_done, 1)
                        if j == 2 and has_ef(it, j):
                            take_oT(it, j, (0,))
                        if has_front(it):
                            guess_norms(it, j)
                        if j == 3 and has_front(it):
                            with at_layer_change(act, it):
                                with first_turn_of_layer(act, it):
                                    split_w1(it)
                                if not isinstance(it, int):
                                    with last_turn_of_layer(act, it), not_last_layer(act, it):
                                        b = a_ring.bank(("qkv", 3, 5))
                                        act.wait_ge(a_full[b], a_ring.nth(("qkv", 3, 5), it))
                                        for c in range(6):
                                            wqkv_high(act, (it >> 3) + 1, c)
                        if j == 3 and has_cd(it, j):
                            exponentials(it, j)
                        if has_ef(it, j):
                            take_oT(it, j, (1,) if j == 2 else (0, 1))
                        if j == 2 and has_ffn(it):
                            b = x_ring.bank(("var", j, 0))
                            act.wait_ge(x_full[b], x_ring.nth(("var", j, 0), it))
                            nc.scalar.activation(lnv[:, :], psum[:, X0 + b, :], ACT.Ln,
                                                 bias=eps[:, :]).then_inc(x_free[b], 1)
                            act.wait_ge(x_free[b], x_ring.nth(("var", j, 0), it))
                            nc.scalar.activation(rstd[:, :], lnv[:, :], ACT.Exp, scale=-0.5).then_inc(rstd_done, 1)
                        if j < 3 and has_cd(it, j):
                            exponentials(it, j)

                nc.scalar.preload_act_table_set(LN_EXP_SET)
                act.wait_ge(zeroed, 1)
                turn(0)
                with act.Fori(1, TURNS) as it:
                    turn(it)
                turn(TURNS)

            @block.gpsimd
            def _(pool):
                def swapped_add(it, j, qk):
                    for half in range(2):
                        own = slice(half * 32, half * 32 + 32)
                        other = slice(32 - half * 32, 64 - half * 32)
                        c = rcos[:, j % 2, 2 * qk:2 * qk + 2, :].rearrange("p c (h e) -> p (c h) e", e=HD)
                        s = rsin[:, 2 * qk:2 * qk + 2, :].rearrange("p c (h e) -> p (c h) e", e=HD)
                        last = nc.gpsimd.tensor_tensor(c[:, :, own], c[:, :, own], s[:, :, other], ALU.add)
                    return last

                def turn(it):
                    for j in range(GT):
                        n = it * GT + j
                        if has_front(it):
                            pool.wait_ge(a_free[a_ring.bank(("qkv", j, 0))], a_ring.nth(("qkv", j, 0), it))
                            pool.wait_ge(a_free[a_ring.bank(("qkv", j, 1))], a_ring.nth(("qkv", j, 1), it))
                            swapped_add(it, j, 0).then_inc(qadd_done, 1)
                            pool.wait_ge(a_free[a_ring.bank(("qkv", j, 2))], a_ring.nth(("qkv", j, 2), it))
                            pool.wait_ge(a_free[a_ring.bank(("qkv", j, 3))], a_ring.nth(("qkv", j, 3), it))
                            swapped_add(it, j, 1).then_inc(kadd_done, 1)
                        if has_front(it):
                            pool.wait_ge(rn_done, known(n + 1))
                            for qk, own, ready in ((0, qadd_done, q_ready), (1, kadd_done, k_ready)):
                                pool.wait_ge(own, known(n + 1))
                                t = rcos[:, j % 2, 2 * qk:2 * qk + 2, :].rearrange("p c (h e) -> p (c h) e", e=HD)
                                nc.gpsimd.tensor_tensor(t, t, rn[:, j % 2, HEADS * qk:HEADS * (qk + 1)].unsqueeze(
                                    2).to_broadcast([P, HEADS, HD]), ALU.mult).then_inc(ready, 1)
                        if has_cd(it, j):
                            pool.wait_ge(rinv_done, known(n))
                            nc.gpsimd.tensor_tensor(p_sb[:, :, :], p_sb[:, :, :],
                                                    rinv[:, :].unsqueeze(2).to_broadcast([P, HEADS, SEQ]),
                                                    ALU.mult).then_inc(pn_done, 1)

                nc.gpsimd.memset(kbd[:, :, :, :], 0.0)
                nc.gpsimd.memset(bd[:, :, :], 0.0)
                nc.gpsimd.memset(xs2[:, :], 0.0).then_inc(pads_zeroed, 1)
                turn(0)
                with pool.Fori(1, TURNS) as it:
                    turn(it)
                turn(TURNS)

            @block.vector
            def _(dve):
                LOWER, UPPER = slice(0, 64), slice(64, 128)

                def after_first(t):
                    return t.rearrange("p (b s) -> p b s", s=SEQ)[:, :, 1:SEQ]

                def before_last(t):
                    return t.rearrange("p (b s) -> p b s", s=SEQ)[:, :, 0:SEQ - 1]

                def shift(dst, src):
                    nc.vector.tensor_copy(dst[LOWER, :], src[LOWER, :])
                    return nc.vector.tensor_copy(after_first(dst[UPPER, :]), before_last(src[UPPER, :]))

                def shift_hi(buf, src):
                    hi = xs_hi[:, buf, :]
                    nc.vector.tensor_copy(hi[LOWER, :], src[LOWER, :])
                    nc.vector.tensor_copy(after_first(hi[UPPER, :]), before_last(src[UPPER, :])).then_inc(xs_hi_done, 1)

                def shift_lo(buf, src, n):
                    hi, lo = xs_hi[:, buf, :].bitcast(F32), xs_lo[:, buf, :]
                    dve.wait_ge(xs_hi_done, n + 1)
                    nc.vector.tensor_tensor(lo[LOWER, :], src[LOWER, :], hi[LOWER, :], ALU.subtract)
                    nc.vector.tensor_tensor(after_first(lo[UPPER, :]), before_last(src[UPPER, :]),
                                            after_first(hi[UPPER, :]), ALU.subtract).then_inc(xs_ready, 1)

                def split_w1(it):
                    dve.wait_ge(w1_hi_done, (it >> 3) + 1)
                    nc.vector.tensor_tensor(w1_lo[:, :], w1_sb[:, :], w1_hi[:, :].bitcast(F32),
                                            ALU.subtract).then_inc(w1_lo_done, 1)

                def tile_of(n):
                    return x[:, bass.ds((n & (TOK // TILE - 1)) * TILE, TILE)]

                def group_of(it):
                    return x[:, bass.ds(((it - 1) & (GROUPS - 1)) * GTOK, GTOK)]

                def transpose_p(it, j):
                    m = it * GT + j - 2
                    dve.wait_ge(pn_done, known(m + 1))
                    dve.wait_ge(bd_done, known(m))
                    nc.vector.transpose(pT[:, :, :], p_sb[:, :, :]).then_inc(pT_done, 1)

                def rotary(it, j, c):
                    n = it * GT + j
                    if c == 0:
                        dve.wait_ge(kadd_done, known(n))
                    b = a_ring.bank(("qkv", j, c))
                    dve.wait_ge(sq_done, known(n * 4 + c + 1))
                    src = psum[:, b, :].rearrange("p (h e) -> p h e", e=HD)
                    for dst, t in ((rcos[:, j % 2, c, :], 2 * (c // 2)), (rsin[:, c, :], 2 * (c // 2) + 1)):
                        last = nc.vector.tensor_tensor(
                            dst.rearrange("p (h e) -> p h e", e=HD), src,
                            tab[:, t:t + 1, :].to_broadcast([P, 8, HD]), ALU.mult)
                    last.then_inc(a_free[b], 1)

                def sum_squares(j, qk):
                    return nc.vector.tensor_reduce(
                        ss[:, j % 2, HEADS * qk:HEADS * (qk + 1)],
                        sq[:, 2 * qk:2 * qk + 2, :].rearrange("p c (h e) -> p (c h) e", e=HD), AX_X, ALU.add)

                def guard_sums(it, j):
                    n = it * GT + j
                    dve.wait_ge(dve_norm, known(n * 3 + 1))
                    nc.vector.tensor_scalar(ssc[:, j % 2, :], ss[:, j % 2, :], 1e-24, None,
                                            ALU.max).then_inc(sums_done, 1)

                def refine_norms(it, j):
                    n = it * GT + j
                    dve.wait_ge(y0_done, known(n + 1))
                    nc.vector.scalar_tensor_tensor(nt_a[:, :], y0[:, j % 2, :], Y_SCALE * Y_SCALE, y0[:, j % 2, :],
                                                   ALU.mult, ALU.mult).then_inc(dve_norm, 1)
                    dve.wait_ge(dve_norm, known(n * 3 + 2))
                    nc.vector.scalar_tensor_tensor(nt_b[:, :], nt_a[:, :], -0.5 * Y_SCALE, ssc[:, j % 2, :],
                                                   ALU.mult, ALU.mult).then_inc(dve_norm, 1)
                    dve.wait_ge(dve_norm, known(n * 3 + 3))
                    nc.vector.scalar_tensor_tensor(rn[:, j % 2, :], nt_b[:, :], 1.5 * Y_SCALE, y0[:, j % 2, :],
                                                   ALU.add, ALU.mult).then_inc(rn_done, 1)

                def subtract_max(it, j):
                    m = it * GT + j - 1
                    s = psum[:, S0:S0 + 2, :].rearrange("p o (h w) -> p (o h) w", w=2 * SEQ)[:, :, 0:SEQ]
                    dve.wait_ge(scores_done, known(m + 1))
                    nc.vector.tensor_reduce(mx[:, :], s, AX_X, ALU.max).then_inc(dve_soft, 1)
                    dve.wait_ge(dve_soft, known(m * 2 + 1))
                    nc.vector.tensor_tensor(s_sb[:, :, :], s, mx[:, :].unsqueeze(2).to_broadcast(
                        [P, HEADS, SEQ]), ALU.subtract).then_inc(s_done, 1)

                def sum_exp(it, j):
                    m = it * GT + j - 1
                    dve.wait_ge(exp_done, known(m + 1))
                    nc.vector.tensor_reduce(sums[:, :], p_sb[:, :, :], AX_X, ALU.add).then_inc(dve_soft, 1)
                    dve.wait_ge(dve_soft, known(m * 2 + 2))
                    nc.vector.reciprocal(rinv[:, :], sums[:, :]).then_inc(rinv_done, 1)

                def add_attention(it, j):
                    m = it * GT + j - 2
                    b = x_ring.bank(("wo", j, 0))
                    dve.wait_ge(x_full[b], x_ring.nth(("wo", j, 0), it))
                    t = tile_of(m)
                    nc.vector.tensor_tensor(t, psum[:, X0 + b, 0:TILE], t, ALU.add).then_inc(x_free[b], 1)

                def take_group(it):
                    for key in (("wo", 0, 0), ("wo", 1, 0)):
                        dve.wait_ge(x_free[x_ring.bank(key)], x_ring.nth(key, it))
                    nc.vector.tensor_copy(lp[:, :].unsqueeze(1), par[:, bass.ds(layer_of(it - 1), 1), :])
                    shift(xs2[:, :], group_of(it)).then_inc(xs2_done, 1)

                def normalize_group(it):
                    dve.wait_ge(rstd_done, known(it))
                    nc.vector.scalar_tensor_tensor(xg[:, :], xc[:, :], lp[:, PG:PG + 1], rstd[:, :],
                                                   ALU.mult, ALU.mult).then_inc(xg_done, 1)
                    dve.wait_ge(xg_done, it)
                    nc.vector.tensor_scalar(xn_hi[:, :], xg[:, :], lp[:, PB:PB + 1], None,
                                            ALU.add).then_inc(xn_hi_done, 1)

                def normalized_low(it):
                    dve.wait_ge(xn_hi_done, it)
                    nc.vector.scalar_tensor_tensor(xn_lo[:, :], xg[:, :], lp[:, PB:PB + 1],
                                                   xn_hi[:, :].bitcast(F32), ALU.add,
                                                   ALU.subtract).then_inc(xn_done, 1)

                def turn(it):
                    for j in range(GT):
                        n = it * GT + j
                        if has_front(it):
                            rotary(it, j, 0)
                            rotary(it, j, 1)
                        if j < 3 and has_ef(it, j):
                            transpose_p(it, j)
                        if j == 2 and has_ffn(it):
                            take_group(it)
                        if j == 3 and has_ffn(it):
                            normalized_low(it)
                        if has_front(it):
                            sum_squares(j, 0)
                            rotary(it, j, 2)
                            rotary(it, j, 3)
                        if j == 3 and has_ef(it, j):
                            transpose_p(it, j)
                        if j == 2 and has_ffn(it):
                            b = x_ring.bank(("mean", j, 0))
                            dve.wait_ge(x_full[b], x_ring.nth(("mean", j, 0), it))
                            nc.vector.tensor_tensor(xc[:, :], xs2[:, :], psum[:, X0 + b, :],
                                                    ALU.subtract).then_inc(x_free[b], 1)
                        if has_front(it):
                            sum_squares(j, 1).then_inc(dve_norm, 1)
                            guard_sums(it, j)
                            b = a_ring.bank(("qkv", j, 0))
                            dve.wait_ge(a_full[b], a_ring.nth(("qkv", j, 0), it))
                            if not (isinstance(it, int) and it == 0):
                                b = a_ring.bank(("down", 3, 0))
                                dve.wait_ge(a_free[b], a_ring.nth(("down", 3, 0), it - 1))
                            shift_hi((j + 1) % 2, tile_of(n + 1))
                        if j == 3 and has_ffn(it):
                            for c in range(3):
                                w = FC[c][1]
                                dve.wait_ge(a_free[a_ring.bank(("up", j, c))], a_ring.nth(("up", j, c), it))
                                b = a_ring.bank(("up", j, 3 + c))
                                dve.wait_ge(a_full[b], a_ring.nth(("up", j, 3 + c), it))
                                nc.vector.scalar_tensor_tensor(h[0:w, c, :], psum[0:w, b, :],
                                                               lp[0:w, PBA + c:PBA + c + 1], gel[0:w, c, :],
                                                               ALU.add, ALU.mult).then_inc(a_free[b], 1)
                        if has_front(it):
                            refine_norms(it, j)
                            shift_lo((j + 1) % 2, tile_of(n + 1), n + 1)
                        if has_cd(it, j):
                            subtract_max(it, j)
                        if j == 2 and has_ffn(it):
                            normalize_group(it)
                        if j == 3 and has_front(it):
                            with at_layer_change(dve, it):
                                with first_turn_of_layer(dve, it):
                                    split_w1(it)
                                if not isinstance(it, int):
                                    with last_turn_of_layer(dve, it), not_last_layer(dve, it):
                                        layer = ((it >> 3) + 1).with_bounds(min_val=0, max_val=LAYERS - 1)
                                        tables(dve, layer)
                                        for c in range(6):
                                            wqkv_low(dve, layer, c)
                        if j < 3 and has_ef(it, j):
                            add_attention(it, j)
                        if has_cd(it, j):
                            sum_exp(it, j)
                        if j == 3 and has_ffn(it):
                            b = a_ring.bank(("down", j, 0))
                            dve.wait_ge(a_full[b], a_ring.nth(("down", j, 0), it))
                            t = group_of(it)
                            nc.vector.scalar_tensor_tensor(t, psum[:, b, :], lp[:, PB2:PB2 + 1], t,
                                                           ALU.add, ALU.add).then_inc(a_free[b], 1)
                        if j == 3 and has_ef(it, j):
                            add_attention(it, j)

                nc.vector.memset(xs_hi[:, :, :].bitcast(F32), 0.0)
                nc.vector.memset(xs_lo[:, :, :].bitcast(F32), 0.0)
                nc.vector.memset(eps[:, :], LN_EPS).then_inc(zeroed, 1)
                dve.wait_ge(zeroed, 1)
                shift_hi(0, x[:, 0:TILE])
                shift_lo(0, x[:, 0:TILE], 0)
                turn(0)
                dve.wait_ge(pads_zeroed, 1)
                with dve.Fori(1, TURNS) as it:
                    turn(it)
                turn(TURNS)

        layers_ctx.close()
        xin = sbuf(root, "xin", [P, TOK])
        xin_loaded = [sem(f"xin_loaded{g}") for g in range(GROUPS)]
        added, stored = sem("added"), sem("stored")
        with nc.Block() as block:
            @block.vector
            def _(dve):
                for g in range(GROUPS):
                    t = slice(g * GTOK, (g + 1) * GTOK)
                    dve.wait_ge(xin_loaded[g], 16)
                    nc.vector.tensor_tensor(x[:, t], x[:, t], xin[:, t], ALU.add).then_inc(added, 1)

            @block.sync
            def _(sp):
                for g in range(GROUPS):
                    t = slice(g * GTOK, (g + 1) * GTOK)
                    sp.dma_start(xin[:, t], xT_in[:, t]).then_inc(xin_loaded[g], 16)
                for g in range(GROUPS):
                    t = slice(g * GTOK, (g + 1) * GTOK)
                    sp.wait_ge(added, g + 1)
                    sp.dma_start(out[:, t], x[:, t]).then_inc(stored, 16)
                sp.wait_ge(stored, GROUPS * 16)


def _rope_tables(np):
    f = np.float32
    half = np.arange(0, HD, 2, dtype=f)
    inv_freq = (f(1.0) / f(10000.0) ** (half / f(HD))).astype(f)
    t = np.arange(SEQ, dtype=f)
    freqs = t[:, None] * inv_freq[None, :]
    freqs = np.concatenate([freqs, freqs], -1)
    base_scale = (half + f(0.4 * HD)) / f(1.4 * HD)
    power = (t - SEQ // 2) / f(16)
    scale = (base_scale[None, :] ** power[:, None]).astype(f)
    scale = np.concatenate([scale, scale], -1)
    sign = np.concatenate([np.ones(HD // 2, f), -np.ones(HD // 2, f)])
    cos, sin = np.cos(freqs).astype(f), (np.sin(freqs) * sign).astype(f)
    tabs = np.stack([cos * scale * f(8), sin * scale * f(8), cos / scale, sin / scale], 1)
    return np.ascontiguousarray(np.tile(tabs, (TB, 1, 1)).astype(f))


def kernel(x, itok_B_0_2, L0_cond_wi, L0_cond_wo, L0_cond_swi, L0_cond_swo, L0_cond_g1, L0_cond_g2,
           L0_ffn_Wqkv, L0_ffn_q_scale, L0_ffn_k_scale, L0_ffn_Wo, L0_ffn_ln_g, L0_ffn_ln_b,
           L0_ffn_W1, L0_ffn_b1, L0_ffn_W2, L0_ffn_b2):
    import numpy as np
    import concourse.bacc as bacc
    from concourse.bass_utils import run_bass_kernel_spmd

    def a(v):
        return np.asarray(v)

    b1 = a(L0_ffn_b1)
    params = np.zeros((P, LAYERS, NPAR), b1.dtype)
    params[:, :, PG], params[:, :, PB], params[:, :, PB2] = a(L0_ffn_ln_g).T, a(L0_ffn_ln_b).T, a(L0_ffn_b2).T
    for c, (off, w) in enumerate(FC):
        params[:w, :, PBA + c] = b1[:, off:off + w].T
        params[:w, :, PBG + c] = b1[:, DI + off:DI + off + w].T
    w2 = np.zeros((3 * P, LAYERS, DIM), np.float32)
    w2[:DI] = a(L0_ffn_W2).transpose(1, 0, 2)
    i, j = np.arange(P)[:, None] % SEQ, np.arange(SEQ)[None, :]
    arrays = {
        "xT_in": a(x).reshape(TOK, DIM).T,
        "label": a(itok_B_0_2),
        "wi": a(L0_cond_wi).transpose(1, 0, 2),
        "wo": a(L0_cond_wo).reshape(EXPERTS, EC, P, DIM).transpose(2, 0, 1, 3),
        "swi": a(L0_cond_swi).transpose(1, 0, 2),
        "swo": a(L0_cond_swo).reshape(SHARED, EC, P, DIM).transpose(2, 0, 1, 3),
        "g1": a(L0_cond_g1).reshape(3, DIM, DIM).transpose(1, 0, 2),
        "g2": a(L0_cond_g2),
        "wqkv": a(L0_ffn_Wqkv).transpose(1, 0, 2),
        "qk_scale": np.stack([a(L0_ffn_q_scale), a(L0_ffn_k_scale)], 1),
        "wout": a(L0_ffn_Wo).reshape(LAYERS, HP, P, DIM).transpose(2, 0, 1, 3),
        "w1": a(L0_ffn_W1).transpose(1, 0, 2),
        "w2": w2.reshape(3, P, LAYERS, DIM).transpose(1, 2, 0, 3),
        "params": params,
        "rope": _rope_tables(np),
        "mask": np.where(j > i, np.float32(NEG), np.float32(0)),
        "ident": np.eye(P, dtype=np.float32),
    }
    nc = bacc.Bacc("TRN2", target_bir_lowering=False, num_devices=1)
    sent, args = {}, []
    for name, v in arrays.items():
        v = np.ascontiguousarray(v)
        sent[f"{name}_dram"] = v
        args.append(nc.dram_tensor(f"{name}_dram", v.shape, mybir.dt.from_np(v.dtype), kind="ExternalInput").ap())
    args.append(nc.dram_tensor("out_dram", (DIM, TOK), F32, kind="ExternalOutput").ap())
    build(nc, *args)
    r = run_bass_kernel_spmd(nc, [sent], core_ids=[0])
    return np.ascontiguousarray(r.results[0]["out_dram"].T).reshape(BATCH, SEQ, DIM)
```
